# Optimizing a Trainium2 kernel written in Bass

```python
import numpy as np
import jax
import jax.numpy as jnp

def _softmax(x, axis=-1):
    return jax.nn.softmax(x, axis=axis)

def _gelu(x):
    return jax.nn.gelu(x, approximate=True)

def _silu(x):
    return jax.nn.silu(x)

def _sigmoid(x):
    return jax.nn.sigmoid(x)

def _layernorm(x, axis=-1, eps=1e-05):
    m = jnp.mean(x, axis=axis, keepdims=True)
    v = jnp.var(x, axis=axis, keepdims=True)
    return (x - m) / jnp.sqrt(v + eps)

def _scatter_add(tgt, idx, src, axis=0):
    return tgt.at[idx].add(src)

def _segment_sum(src, seg, n):
    return jax.ops.segment_sum(src, seg, n)
kernel_name = 'mk_flamingo_gated_d1_seqx_r8_644ce1'

def setup_inputs(seed: int=0):
    np.random.seed(seed)
    _w = jnp.asarray

    def _rec_inputs():
        import jax
        import jax.numpy as jnp
        _rk = jax.random.key(seed)
        x = 7.22e-05 + 1 * jax.random.normal(jax.random.fold_in(_rk, 1), (32, 64, 128), jnp.float32)
        _lenS = 64 - jax.random.randint(jax.random.fold_in(_rk, 7), (32,), 0, max(1, 64 // 4) + 1, jnp.int32)
        _lenS2 = 64 - jax.random.randint(jax.random.fold_in(_rk, 8), (32,), 0, max(1, 64 // 4) + 1, jnp.int32)
        _ctx_1024P = jax.random.normal(jax.random.fold_in(_rk, 11), (32, 16, 128), jnp.float32)
        _ctx_1024c = jax.random.dirichlet(jax.random.fold_in(_rk, 511), 0.3 * jnp.ones((16,), jnp.float32), (32, 64))
        _ctx_1024t = jnp.einsum('bsk,bkd->bsd', _ctx_1024c, _ctx_1024P)
        _ctx_1024t = _ctx_1024t * jax.lax.rsqrt(jnp.mean(jnp.square(_ctx_1024t)) + 1e-12) * 0.953939
        ctx_1024 = 4.13588e-05 + 0.999923 * (_ctx_1024t + 0.3 * jax.random.normal(jax.random.fold_in(_rk, 611), (32, 64, 128), jnp.float32))
        itok_BxS2_0_99 = jax.random.randint(jax.random.fold_in(_rk, 12), (32, 64), 0, 100, jnp.int32)
        _g = jax.random.normal(jax.random.fold_in(_rk, 9001), (2, 1), jnp.float32)
        _g = jnp.sign(_g) * jnp.maximum(jnp.abs(_g), 1.0) + (_g == 0) * 1.0
        g_xattn = _g[0]
        g_ffn = _g[1]
        return (x, ctx_1024, itok_BxS2_0_99, g_xattn, g_ffn)
    x, ctx_1024, itok_BxS2_0_99, g_xattn, g_ffn = _rec_inputs()

    def _L0_xattn_setup():
        import jax, jax.numpy as jnp
        import numpy as np
        B, S, D = (4, 256, 128)
        H = 16
        HD = D // H
        NEG = -1000000000.0
        key = jax.random.key(seed)
        ks = jax.random.split(key, 8)
        x = jax.random.normal(ks[0], (B, S, D), dtype=jnp.float32)
        y = jax.random.normal(ks[1], (B, S, D), dtype=jnp.float32)
        log_seqs = jax.random.randint(ks[2], (B, S), 0, 100, dtype=jnp.int64)
        sc = 1.0 / np.sqrt(D)
        Wq = jax.random.normal(ks[3], (D, D), dtype=jnp.float32) * sc
        Wk = jax.random.normal(ks[4], (D, D), dtype=jnp.float32) * sc
        Wv = jax.random.normal(ks[5], (D, D), dtype=jnp.float32) * sc
        Wo = jax.random.normal(ks[6], (D, D), dtype=jnp.float32) * sc
        bo = jnp.zeros((D,), dtype=jnp.float32)
        return {'x': x, 'y': y, 'log_seqs': log_seqs, 'pad_id': 0, 'Wq': Wq, 'Wk': Wk, 'Wv': Wv, 'Wo': Wo, 'bo': bo}
    _L0_xattn_all = _L0_xattn_setup()
    _L0_xattn_in = {k: v for k, v in _L0_xattn_all.items() if k in ('Wq', 'Wk', 'Wv', 'Wo', 'bo')}
    del _L0_xattn_all

    def _L0_ffn_setup():
        import jax, jax.numpy as jnp
        import numpy as np
        from jax import lax
        TOP_K = 4
        N_GROUP = 4
        TOPK_GROUP = 2
        ROUTED_SCALE = 2.5
        NEG_INF = -1000000000.0

        def _route(xf, router_weight, router_bias):
            T = xf.shape[0]
            E = router_weight.shape[0]
            logits = xf @ router_weight.T
            scores = jax.nn.sigmoid(logits)
            s_choice = scores + router_bias
            per_group = E // N_GROUP
            sg = s_choice.reshape(T, N_GROUP, per_group)
            group_scores = lax.top_k(sg, 2)[0].sum(-1)
            _, gidx = lax.top_k(group_scores, TOPK_GROUP)
            gmask = jnp.zeros((T, N_GROUP), dtype=bool).at[jnp.arange(T)[:, None], gidx].set(True)
            masked = jnp.where(gmask[:, :, None], sg, NEG_INF).reshape(T, E)
            _, topk_idx = lax.top_k(masked, TOP_K)
            w = jnp.take_along_axis(scores, topk_idx, axis=1)
            w = w / (w.sum(-1, keepdims=True) + 1e-20) * ROUTED_SCALE
            combine = jnp.zeros((T, E), dtype=xf.dtype).at[jnp.arange(T)[:, None], topk_idx].add(w)
            return combine
        key = jax.random.key(seed)
        ks = jax.random.split(key, 6)
        B, S, H, I, E = (2, 256, 128, 64, 16)
        x = jax.random.normal(ks[0], (B, S, H), dtype=jnp.float32)
        router_weight = jax.random.normal(ks[1], (E, H), dtype=jnp.float32) * 0.02
        router_bias = jnp.zeros((E,), dtype=jnp.float32)
        w_gate = jax.random.normal(ks[2], (E, I, H), dtype=jnp.float32) * 0.02
        w_up = jax.random.normal(ks[3], (E, I, H), dtype=jnp.float32) * 0.02
        w_down = jax.random.normal(ks[4], (E, H, I), dtype=jnp.float32) * 0.02
        return {'x': x, 'router_weight': router_weight, 'router_bias': router_bias, 'w_gate': w_gate, 'w_up': w_up, 'w_down': w_down}
    _L0_ffn_all = _L0_ffn_setup()
    _L0_ffn_in = {k: v for k, v in _L0_ffn_all.items() if k in ('router_weight', 'router_bias', 'w_gate', 'w_up', 'w_down')}
    del _L0_ffn_all
    return {'x': x, 'ctx_1024': ctx_1024, 'itok_BxS2_0_99': itok_BxS2_0_99, 'g_xattn': g_xattn, 'g_ffn': g_ffn, 'L0_xattn_Wq': _L0_xattn_in['Wq'], 'L0_xattn_Wk': _L0_xattn_in['Wk'], 'L0_xattn_Wv': _L0_xattn_in['Wv'], 'L0_xattn_Wo': _L0_xattn_in['Wo'], 'L0_xattn_bo': _L0_xattn_in['bo'], 'L0_ffn_router_weight': _L0_ffn_in['router_weight'], 'L0_ffn_router_bias': _L0_ffn_in['router_bias'], 'L0_ffn_w_gate': _L0_ffn_in['w_gate'], 'L0_ffn_w_up': _L0_ffn_in['w_up'], 'L0_ffn_w_down': _L0_ffn_in['w_down']}

def reference(x, ctx_1024, itok_BxS2_0_99, g_xattn, g_ffn, L0_xattn_Wq, L0_xattn_Wk, L0_xattn_Wv, L0_xattn_Wo, L0_xattn_bo, L0_ffn_router_weight, L0_ffn_router_bias, L0_ffn_w_gate, L0_ffn_w_up, L0_ffn_w_down):
    import jax
    import jax.numpy as jnp

    def _L0_xattn_ref(x, y, log_seqs, pad_id, Wq, Wk, Wv, Wo, bo):
        import jax, jax.numpy as jnp
        import numpy as np
        B, S, D = (4, 256, 128)
        H = 16
        HD = D // H
        NEG = -1000000000.0
        b = x.shape[0]
        q = (x @ Wq).reshape(b, -1, H, HD).transpose(0, 2, 1, 3)
        k = (y @ Wk).reshape(b, -1, H, HD).transpose(0, 2, 1, 3)
        v = (y @ Wv).reshape(b, -1, H, HD).transpose(0, 2, 1, 3)
        mask = (log_seqs == pad_id)[:, None, None, :]
        scores = jnp.einsum('bhqd,bhkd->bhqk', q, k)
        scores = jnp.where(mask, NEG, scores)
        probs = jax.nn.softmax(scores / np.sqrt(HD), axis=-1)
        attn = jnp.einsum('bhqk,bhkd->bhqd', probs, v)
        attn = attn.transpose(0, 2, 1, 3).reshape(b, -1, H * HD)
        return attn @ Wo + bo

    def _L0_ffn_ref(x, router_weight, router_bias, w_gate, w_up, w_down):
        import jax, jax.numpy as jnp
        import numpy as np
        from jax import lax
        TOP_K = 4
        N_GROUP = 4
        TOPK_GROUP = 2
        ROUTED_SCALE = 2.5
        NEG_INF = -1000000000.0

        def _route(xf, router_weight, router_bias):
            T = xf.shape[0]
            E = router_weight.shape[0]
            logits = xf @ router_weight.T
            scores = jax.nn.sigmoid(logits)
            s_choice = scores + router_bias
            per_group = E // N_GROUP
            sg = s_choice.reshape(T, N_GROUP, per_group)
            group_scores = lax.top_k(sg, 2)[0].sum(-1)
            _, gidx = lax.top_k(group_scores, TOPK_GROUP)
            gmask = jnp.zeros((T, N_GROUP), dtype=bool).at[jnp.arange(T)[:, None], gidx].set(True)
            masked = jnp.where(gmask[:, :, None], sg, NEG_INF).reshape(T, E)
            _, topk_idx = lax.top_k(masked, TOP_K)
            w = jnp.take_along_axis(scores, topk_idx, axis=1)
            w = w / (w.sum(-1, keepdims=True) + 1e-20) * ROUTED_SCALE
            combine = jnp.zeros((T, E), dtype=xf.dtype).at[jnp.arange(T)[:, None], topk_idx].add(w)
            return combine
        B, S, H = x.shape
        E = w_gate.shape[0]
        xf = x.reshape(-1, H)
        combine = _route(xf, router_weight, router_bias)
        out = jnp.zeros_like(xf)
        for e in range(E):
            g = xf @ w_gate[e].T
            u = xf @ w_up[e].T
            y_e = jax.nn.silu(g) * u @ w_down[e].T
            out = out + combine[:, e:e + 1] * y_e
        return out.reshape(B, S, H)
    x = x + jnp.tanh(g_xattn[0]) * _L0_xattn_ref(_layernorm(x, axis=-1), ctx_1024, itok_BxS2_0_99, 0, L0_xattn_Wq, L0_xattn_Wk, L0_xattn_Wv, L0_xattn_Wo, L0_xattn_bo)
    x = x + jnp.tanh(g_ffn[0]) * _L0_ffn_ref(_layernorm(x, axis=-1), L0_ffn_router_weight, L0_ffn_router_bias, L0_ffn_w_gate, L0_ffn_w_up, L0_ffn_w_down)
    return x

_drawn_inputs = setup_inputs


def setup_inputs(seed=0):
    import zlib

    import numpy as np

    out = dict(_drawn_inputs(seed))
    spreads = {'L0_xattn_bo': (0.0, 0.1), 'L0_ffn_router_bias': (0.0, 0.8)}
    factors = {'L0_ffn_router_weight': 8.0,
     'L0_ffn_w_gate': 8.0,
     'L0_ffn_w_up': 8.0,
     'L0_ffn_w_down': 8.0}
    for name, (base, spread) in spreads.items():
        noise = np.random.default_rng([zlib.crc32(name.encode()), seed]).standard_normal(out[name].shape)
        drawn = base * np.exp(spread * noise) if base else spread * noise
        out[name] = jnp.asarray(drawn.astype(out[name].dtype))
    for name, factor in factors.items():
        out[name] = (out[name] * factor).astype(out[name].dtype)
    return out
```

```python
from contextlib import ExitStack

import numpy as np

import concourse.bass as bass
from concourse import mybir

F32 = mybir.dt.float32
F32R = mybir.dt.float32r
BF16 = mybir.dt.bfloat16
I32 = mybir.dt.int32
ALU = mybir.AluOpType
ACT = mybir.ActivationFunctionType
AX = mybir.AxisListType

P = 128
B, S, D = 32, 64, 128
H, HD = 16, 8
E, I = 16, 64
NT = B * S // P
HH = H // 2
HP = H // 2
EP = E // 2
GT = 4
NG = NT // GT
GN = GT * P
NEG = -1000000000.0
NPIECE = 3
LN_EPS = 1e-5
SM_SCALE = float(1.0 / np.sqrt(HD))
GROUPS, PER_GROUP, TOP_K = 4, 4, 4
FIRST_STEP = 5
ROUTED_SCALE = 2.5


def neg_pieces():
    rest, out = np.float32(NEG), []
    for _ in range(NPIECE):
        piece = (rest.reshape(1).view(np.uint32) & np.uint32(0xFFFF0000)).view(np.float32)[0]
        out.append(piece)
        rest = np.float32(rest - piece)
    assert rest == 0
    return out


def constants():
    ident = np.eye(P, dtype=np.float32)
    p = np.arange(P)
    head_mask = ((p[:, None] % 64) // HD == np.arange(HH)[None, :]).astype(np.float32)
    batch_rows = np.zeros((P, P), np.float32)
    neg_col = np.zeros((P, 1), np.float32)
    for b in range(2):
        for i, v in enumerate(neg_pieces()):
            batch_rows[NPIECE * b + i, 64 * b:64 * b + 64] = 1.0
            neg_col[NPIECE * b + i] = v
    expert_rows = np.zeros((P, EP, P), np.float32)
    for q in range(EP):
        for j in range(2):
            for part in range(2):
                expert_rows[16 * part + 2 * q + j, q, 64 * j:64 * j + 64] = 1.0
    g, j = np.arange(GROUPS)[:, None], np.arange(GROUPS)[None, :]
    before = np.broadcast_to((j < g).astype(np.float32), (P, GROUPS, GROUPS))
    after = np.broadcast_to((j > g).astype(np.float32), (P, GROUPS, GROUPS))
    return {"c_ident": ident, "c_head_mask": head_mask, "c_batch_rows": batch_rows, "c_neg_col": neg_col,
            "c_expert_rows": expert_rows.reshape(P, EP * P),
            "c_group_order": np.ascontiguousarray(np.stack([before, after], 1).reshape(P, -1))}


def build(nc, a, out):
    ctx = ExitStack()
    with ctx:
        def sb(name, shape, dt=F32):
            return ctx.enter_context(nc.sbuf_tensor(name, shape, dt))

        def sem(name):
            return ctx.enter_context(nc.semaphore(name))

        ident = sb("ident", [P, P])
        head_mask = sb("head_mask", [P, HH])
        batch_rows_f = sb("batch_rows_f", [P, P])
        batch_rows = sb("batch_rows", [P, P], BF16)
        neg_col = sb("neg_col", [P, 1])
        wq = sb("wq", [P, P])
        wk = sb("wk", [P, P])
        wv = sb("wv", [P, P])
        wo = sb("wo", [P, P])
        bo_rows = sb("bo_rows", [P, P])
        gates = sb("gates", [P, 2])
        tgates = sb("tgates", [P, 2])
        gbo = sb("gbo", [P, P])
        rwT = sb("rwT", [P, E])
        rbias = sb("rbias", [P, E])
        group_order = sb("group_order", [P, 2, GROUPS, GROUPS])
        expert_rows_f = sb("expert_rows_f", [P, EP, P])
        expert_rows = sb("expert_rows", [P, EP, P], F32R)
        wg_f = sb("wg_f", [P, E * I])
        wu_f = sb("wu_f", [P, E * I])
        wg_hi = sb("wg_hi", [P, E * I], F32R)
        wg_lo = sb("wg_lo", [P, E * I], F32R)
        wu_hi = sb("wu_hi", [P, E * I], F32R)
        wu_lo = sb("wu_lo", [P, E * I], F32R)
        wd = sb("wd", [P, EP, D])

        x_all = sb("x_all", [P, NT, D])
        x1_all = sb("x1_all", [P, NT, D])
        stats = sb("stats", [P, NT, 6])
        mv1 = sb("mv1", [P, NT, 2])
        var1 = sb("var1", [P, NT])
        rstd1 = sb("rstd1", [P, NT])
        minus_half = sb("minus_half", [P, NT])
        keys_tok = sb("keys_tok", [P, NT, S], I32)
        keep = sb("keep", [P, NT, S])
        neg_tok = sb("neg_tok", [P, NT, S], I32)
        neg_rows = sb("neg_rows", [P, NT, S], BF16)
        ctxT = sb("ctxT", [P, 2, P])
        xh = sb("xh", [P, 2, D])
        xT = sb("xT", [P, P])
        q_blk = sb("q_blk", [P, 2, 2, P])
        kT = sb("kT", [P, 2, S])
        k_exp = sb("k_exp", [P, 2, 2, HH, S])
        v_blk = sb("v_blk", [P, 2, 2, HP, 32])
        s_max = sb("s_max", [P, 2, H])
        s_sub = sb("s_sub", [P, 2, H, S])
        probs = sb("probs", [P, 2, H * S])
        pT = sb("pT", [P, HP, P])
        oT = sb("oT", [P, 2, P])
        o_inv = sb("o_inv", [P, HP, 2])
        o_tok = sb("o_tok", [P, HP, 2, HD])
        onT = sb("onT", [P, P])
        stats2 = sb("stats2", [P, 6])
        mv2 = sb("mv2", [P, 2, 2])
        var2 = sb("var2", [P, 2])
        rstd2 = sb("rstd2", [P, 2])
        xh2 = sb("xh2", [P, 2, D])
        x2T = sb("x2T", [P, P])
        x2_hi = sb("x2_hi", [P, NT * P], F32R)
        x2_lo = sb("x2_lo", [P, NT * P], F32R)

        exp_logit = sb("exp_logit", [P, NT, E])
        r_den = sb("r_den", [P, NT, E])
        score = sb("score", [P, NT, E])
        choice = sb("choice", [P, NT, E])
        pair_hi = sb("pair_hi", [P, NT * GROUPS, 2])
        pair_lo = sb("pair_lo", [P, NT * GROUPS, 2])
        top1 = sb("top1", [P, NT * GROUPS])
        low_hi = sb("low_hi", [P, NT * GROUPS])
        hi_low = sb("hi_low", [P, NT * GROUPS])
        top2 = sb("top2", [P, NT * GROUPS])
        g_score = sb("g_score", [P, NT, GROUPS])
        g_ge = sb("g_ge", [P, NT, GROUPS, GROUPS])
        g_gt = sb("g_gt", [P, NT, GROUPS, GROUPS])
        g_rank = sb("g_rank", [P, NT, GROUPS])
        g_keep = sb("g_keep", [P, NT, GROUPS])
        g_neg = sb("g_neg", [P, NT, GROUPS])
        masked = sb("masked", [P, NT, E])
        best = sb("best", [P, NT, 8])
        rest = sb("rest", [P, NT, E])
        chosen = sb("chosen", [P, NT, E])
        w_sel = sb("w_sel", [P, NT, E])
        w_sum = sb("w_sum", [P, NT])
        w_inv = sb("w_inv", [P, NT])
        comb = sb("comb", [P, NT, E])
        comb_hi = sb("comb_hi", [P, NT, E], F32R)
        comb_parts = sb("comb_parts", [P, NT, 2, E])
        combT = sb("combT", [P, NT * P], F32R)

        silu_g = sb("silu_g", [P, 2, GN])
        gu = sb("gu", [P, 2, GN])
        hid = sb("hid", [P, 2, GN])
        y_out = sb("y_out", [P, NT, D])

        ps = [ctx.enter_context(nc.psum_tensor(f"ps_scores{i}", [P, 2, 512], F32)) for i in range(2)]
        ps_pT = [ctx.enter_context(nc.psum_tensor(f"ps_pT{i}", [P, 4, P], F32)) for i in range(2)]
        ps_front = ctx.enter_context(nc.psum_tensor("ps_front", [P, 512], F32))
        ps_back = ctx.enter_context(nc.psum_tensor("ps_back", [P, 512], F32))
        f_xT, f_kT = ps_front[:, 0:128], ps_front[:, 128:256]
        f_v, f_qT = ps_front[:, 256:384], ps_front[:, 384:512]
        ps_gate = [ps[0][:, 0, :], ps[0][:, 1, :]]
        ps_up = [ps[1][:, 0, :], ps[1][:, 1, :]]
        ps_comb = [ps_pT[0][:, :, :].rearrange("p a b -> p (a b)"), ps_pT[1][:, :, :].rearrange("p a b -> p (a b)")]
        ps_y = ps_back

        ld_front, ld_mask, ld_back, ld_moe = sem("ld_front"), sem("ld_mask"), sem("ld_back"), sem("ld_moe")
        ld_x = [sem(f"ld_x{c}") for c in range(NG)]
        ld_ctx = [sem(f"ld_ctx{p}") for p in range(2)]
        zeroed = sem("zeroed")
        chain = sem("chain")
        var1_ready, rstd1_ready = sem("var1_ready"), sem("rstd1_ready")
        batch_rows_ready, neg_ready, tanh_ready, gbo_ready = (
            sem("batch_rows_ready"), sem("neg_ready"), sem("tanh_ready"), sem("gbo_ready"))
        xh_ready, xk_done, v_done, xT_ready, kT_ready, v_ready = (
            sem("xh_ready"), sem("xk_done"), sem("v_done"), sem("xT_ready"), sem("kT_ready"), sem("v_ready"))
        q_done, q_ready, k_exp_ready, xbo_ready = sem("q_done"), sem("q_ready"), sem("k_exp_ready"), sem("xbo_ready")
        scores_done, max_ready, sub_ready, probs_ready = (
            sem("scores_done"), sem("max_ready"), sem("sub_ready"), sem("probs_ready"))
        pT_done, pT_ready = sem("pT_done"), sem("pT_ready")
        pv_done, oT_ready, o_turned, o_inv_ready, o_tok_ready = (
            sem("pv_done"), sem("oT_ready"), sem("o_turned"), sem("o_inv_ready"), sem("o_tok_ready"))
        on_turned, onT_ready, wo_done, x1_ready = sem("on_turned"), sem("onT_ready"), sem("wo_done"), sem("x1_ready")
        st2_ready, mv2_ready, var2_ready, rstd2_ready, xh2_ready = (
            sem("st2_ready"), sem("mv2_ready"), sem("var2_ready"), sem("rstd2_ready"), sem("xh2_ready"))
        x2_turned, x2T_ready, x2hi_ready, x2lo_ready, logits_done, elog_ready = (
            sem("x2_turned"), sem("x2T_ready"), sem("x2hi_ready"), sem("x2lo_ready"), sem("logits_done"), sem("elog_ready"))
        whi_ready, wlo_ready = sem("whi_ready"), sem("wlo_ready")
        parts_ready, parts_turned, combT_ready = sem("parts_ready"), sem("parts_turned"), sem("combT_ready")
        gate_done, up_done, comb_done, silu_ready, gu_ready, hid_ready, down_done = (
            sem("gate_done"), sem("up_done"), sem("comb_done"), sem("silu_ready"), sem("gu_ready"),
            sem("hid_ready"), sem("down_done"))
        y_ready, y_sent = sem("y_ready"), sem("y_sent")

        x_dram = a["x"].rearrange("b s d -> (b s) d").rearrange("(t p) d -> p t d", p=P)
        out_dram = out.rearrange("b s d -> (b s) d").rearrange("(t p) d -> p t d", p=P)
        ctx_dram = a["ctxT"].rearrange("d (t p) -> d t p", p=P)
        tok_dram = a["itok"].rearrange("(t b) k -> b t k", b=2)

        def v_pair(w, h2):
            return w[:, :].rearrange("p (n h d) -> p n h d", h=2, d=HD)[:, :, h2, :]

        block = ctx.enter_context(nc.Block())

        def pipeline(eng, step):
            for s in range(-1, FIRST_STEP):
                step(s)
            with eng.Fori(0, (NT - 1 - FIRST_STEP) // 2) as i:
                for u in range(2):
                    step(2 * i + (FIRST_STEP + u), 1 - u)
            for s in range(NT - 1, NT + 3):
                step(s)

        def live(s, d):
            return not isinstance(s, int) or 0 <= s + d < NT

        def at(s, par, d):
            return s + d, ((s if par is None else par) + d) % 2

        def past(t, k):
            return not isinstance(t, int) or t >= k

        @block.sync
        def _(sp):
            sp.dma_start(x_all[:, 0:GT, :], x_dram[:, 0:GT, :]).then_inc(ld_x[0], 16)
            for dst, src in ((ident, a["c_ident"]), (wk, a["wk"]), (wv, a["wv"]), (wq, a["wq"]),
                             (head_mask, a["c_head_mask"])):
                sp.dma_start(dst[:, :], src).then_inc(ld_front, 16)
            for c in range(1, NG):
                sp.dma_start(x_all[:, GT * c:GT * c + GT, :], x_dram[:, GT * c:GT * c + GT, :]).then_inc(ld_x[c], 16)

            def step(s, par=None):
                if live(s, 1):
                    t, p = at(s, par, 1)
                    if past(t, 2):
                        sp.wait_ge(v_done, t - 1)
                    sp.dma_start(ctxT[:, p, :], ctx_dram[:, bass.ds(t, 1), :].squeeze(1)
                                 if not isinstance(t, int) else ctx_dram[:, t, :]).then_inc(ld_ctx[p], 16)

            pipeline(sp, step)
            with sp.Fori(0, NG) as g:
                sp.wait_ge(y_ready, g + 1)
                sp.dma_start(out_dram[:, bass.ds(GT * g, GT), :], y_out[:, bass.ds(GT * g, GT), :]).then_inc(y_sent, 16)
            sp.wait_ge(y_sent, 16 * NG)

        @block.scalar
        def _(act):
            for b in range(2):
                act.dma_start(keys_tok[64 * b:64 * b + 64, :, :], tok_dram[b].partition_broadcast(64)).then_inc(ld_mask, 16)
                act.dma_start(neg_tok[NPIECE * b:NPIECE * b + NPIECE, :, :],
                              tok_dram[b].partition_broadcast(NPIECE)).then_inc(ld_mask, 16)
            act.dma_start(neg_col[:, :], a["c_neg_col"]).then_inc(ld_mask, 16)
            act.dma_start(batch_rows_f[:, :], a["c_batch_rows"]).then_inc(ld_mask, 16)
            act.dma_start(gates[:, 0:1], a["g_xattn"].partition_broadcast(P)).then_inc(ld_back, 16)
            act.dma_start(gates[:, 1:2], a["g_ffn"].partition_broadcast(P)).then_inc(ld_back, 16)
            act.dma_start(bo_rows[:, :], a["bo"].partition_broadcast(P)).then_inc(ld_back, 16)
            act.dma_start(wo[:, :], a["wo"]).then_inc(ld_back, 16)
            act.dma_start(rwT[:, :], a["rwT"]).then_inc(ld_back, 16)
            act.dma_start(rbias[:, :], a["rbias"].partition_broadcast(P)).then_inc(ld_back, 16)
            act.dma_start(group_order[:, :, :, :], a["c_group_order"].rearrange("p (o g j) -> p o g j", o=2, g=GROUPS)
                          ).then_inc(ld_back, 16)
            act.dma_start(wg_f[:, :], a["wgT"]).then_inc(ld_moe, 16)
            act.dma_start(wu_f[:, :], a["wuT"]).then_inc(ld_moe, 16)
            act.dma_start(wd[:, :, :], a["wdT"].rearrange("(q p) d -> p q d", p=P)).then_inc(ld_moe, 16)
            act.dma_start(expert_rows_f[:, :, :], a["c_expert_rows"].rearrange("p (q c) -> p q c", q=EP)
                          ).then_inc(ld_moe, 16)
            act.wait_ge(ld_back, 16 * 7)
            nc.scalar.activation(tgates[:, :], gates[:, :], ACT.Tanh).then_inc(tanh_ready, 1)

            def step(s, par=None):
                if live(s, -1):
                    t, p = at(s, par, -1)
                    for h in range(2):
                        act.wait_ge(sub_ready, 2 * t + h + 1)
                        if past(t, 2):
                            act.wait_ge(pT_done, 2 * (t - 2) + h + 1)
                        nc.scalar.activation(probs[:, p, 512 * h:512 * h + 512],
                                             s_sub[:, p, HH * h:HH * h + HH, :].rearrange("p h k -> p (h k)"),
                                             ACT.Exp, scale=SM_SCALE).then_inc(probs_ready, 1)
                if live(s, 1):
                    t, p = at(s, par, 1)
                    act.wait_ge(xk_done, t + 1)
                    nc.scalar.copy(xT[:, :], f_xT).then_inc(xT_ready, 1)
                if live(s, -2):
                    t, p = at(s, par, -2)
                    act.wait_ge(on_turned, t + 1)
                    nc.scalar.copy(onT[:, :], ps_back[:, 256:384]).then_inc(onT_ready, 1)
                if live(s, -1):
                    t, p = at(s, par, -1)
                    act.wait_ge(pT_done, 2 * t + 1)
                    if past(t, 1):
                        act.wait_ge(pv_done, t)
                    nc.scalar.copy(pT[:, 0:4, :], ps_pT[0][:, :, :]).then_inc(pT_ready, 1)
                if live(s, 1):
                    t, p = at(s, par, 1)
                    act.wait_ge(q_done, t + 1)
                    if not past(t, 2):
                        act.wait_ge(zeroed, 1)
                    for b in range(2):
                        r = slice(64 * b, 64 * b + 64)
                        nc.scalar.copy(q_blk[r, p, :, 64 * b:64 * b + 64],
                                       f_qT[r, :].rearrange("p (a q) -> p a q", a=2)).then_inc(q_ready, 1)
                if live(s, -1):
                    t, p = at(s, par, -1)
                    act.wait_ge(pT_done, 2 * t + 2)
                    nc.scalar.copy(pT[:, 4:8, :], ps_pT[1][:, :, :]).then_inc(pT_ready, 1)
                if live(s, -3):
                    t, p = at(s, par, -3)
                    act.wait_ge(x2_turned, t + 1)
                    nc.scalar.copy(x2T[:, :], ps_back[:, 0:128]).then_inc(x2T_ready, 1)
                    act.wait_ge(x2T_ready, t + 1)
                    nc.scalar.copy(x2_hi[:, bass.ts(t, P)], x2T[:, :]).then_inc(x2hi_ready, 1)
                    act.wait_ge(logits_done, t + 1)
                    nc.scalar.activation(exp_logit[:, t, :] if isinstance(t, int) else
                                         exp_logit[:, bass.ds(t, 1), :].squeeze(1),
                                         ps_back[:, 128:128 + E], ACT.Exp, scale=-1.0).then_inc(elog_ready, 1)
                if live(s, -1):
                    t, p = at(s, par, -1)
                    act.wait_ge(pv_done, t + 1)
                    nc.scalar.copy(oT[:, :, :].rearrange("p a c -> p (a c)"), ps_back[:, 0:256]).then_inc(oT_ready, 1)

            pipeline(act, step)
            for g in range(NG):
                act.wait_ge(parts_turned, g + 1)
                nc.scalar.copy(combT[0:2 * E, GN * g:GN * g + GN], (ps_gate + ps_up)[g][0:2 * E, :]).then_inc(combT_ready, 1)

            def silu(g, q):
                n = EP * g + q
                act.wait_ge(gate_done, n + 1)
                if past(n, 2):
                    act.wait_ge(gu_ready, n - 1)
                nc.scalar.activation(silu_g[:, q % 2, :], ps_gate[q % 2], ACT.Silu).then_inc(silu_ready, 1)

            for q in range(EP):
                silu(0, q)
            with act.Fori(1, NG) as g:
                for q in range(EP):
                    silu(g, q)

        @block.gpsimd
        def _(pool):
            nc.gpsimd.memset(minus_half[:, :], -0.5).then_inc(zeroed, 1)
            pool.wait_ge(zeroed, 4)
            pool.wait_ge(var1_ready, 1)
            nc.gpsimd.tensor_tensor(rstd1[:, :], var1[:, :], minus_half[:, :], ALU.pow).then_inc(rstd1_ready, 1)
            pool.wait_ge(ld_front, 16 * 5)

            def step(s, par=None):
                if live(s, 1):
                    t, p = at(s, par, 1)
                    pool.wait_ge(kT_ready, t + 1)
                    if past(t, 2):
                        pool.wait_ge(scores_done, 2 * (t - 2) + 2)
                    nc.gpsimd.tensor_tensor(k_exp[:, p, :, :, :],
                                            kT[:, :, :].unsqueeze(2).broadcast_to([P, 2, HH, S]),
                                            head_mask[:, :].unsqueeze(1).unsqueeze(3).broadcast_to([P, 2, HH, S]),
                                            ALU.mult).then_inc(k_exp_ready, 1)
                    if not past(t, 1):
                        pool.wait_ge(gbo_ready, 1)
                    row = slice(t, t + 1) if isinstance(t, int) else bass.ds(t, 1)
                    nc.gpsimd.tensor_tensor(x1_all[:, row, :].squeeze(1), x_all[:, row, :].squeeze(1), gbo[:, :],
                                            ALU.add).then_inc(xbo_ready, 1)
                if live(s, -2):
                    t, p = at(s, par, -2)
                    pool.wait_ge(var2_ready, t + 1)
                    nc.gpsimd.tensor_tensor(rstd2[:, p:p + 1], var2[:, p:p + 1], minus_half[:, 0:1],
                                            ALU.pow).then_inc(rstd2_ready, 1)
                if live(s, -3):
                    t, p = at(s, par, -3)
                    pool.wait_ge(x2hi_ready, t + 1)
                    nc.gpsimd.tensor_tensor(x2_lo[:, bass.ts(t, P)], x2T[:, :], x2_hi[:, bass.ts(t, P)].bitcast(F32),
                                            ALU.subtract).then_inc(x2lo_ready, 1)

            pipeline(pool, step)

        @block.vector
        def _(dve):
            nc.vector.memset(q_blk[:, :, :, :], 0.0).then_inc(zeroed, 1)
            nc.vector.memset(v_blk[:, :, :, :, :], 0.0).then_inc(zeroed, 1)
            nc.vector.memset(neg_rows[:, :, :].rearrange("p t k -> p (t k)"), 0.0).then_inc(zeroed, 1)
            dve.wait_ge(zeroed, 4)
            nc.vector.memset(v_blk[0:64, :, :, :, 16:17], 1.0).then_inc(zeroed, 1)
            nc.vector.memset(v_blk[64:128, :, :, :, 17:18], 1.0).then_inc(zeroed, 1)
            links = [0]

            def link(instruction):
                links[0] += 1
                instruction.then_inc(chain, 1)
                dve.wait_ge(chain, links[0])

            for c in range(NG):
                dve.wait_ge(ld_x[c], 16)
                for t in range(GT * c, GT * c + GT):
                    last = nc.vector.bn_stats(stats[:, t, :], x_all[:, t, :])
            link(last)
            for t in range(NT):
                last = nc.vector.bn_aggr(mv1[:, t, :], stats[:, t, :])
            link(last)
            nc.vector.tensor_scalar(var1[:, :], mv1[:, :, 1], LN_EPS, None, ALU.add).then_inc(var1_ready, 1)
            dve.wait_ge(ld_mask, 16 * 6)
            nc.vector.tensor_copy(batch_rows[:, :], batch_rows_f[:, :]).then_inc(batch_rows_ready, 1)
            link(nc.vector.tensor_scalar(keep[:, :, :], keys_tok[:, :, :], 0.0, None, ALU.not_equal))
            nr = 2 * NPIECE
            nc.vector.tensor_scalar(neg_rows[0:nr, :, :], neg_tok[0:nr, :, :], 0.0, neg_col[0:nr, :],
                                    ALU.is_equal, ALU.mult).then_inc(neg_ready, 1)
            dve.wait_ge(tanh_ready, 1)
            nc.vector.tensor_scalar(gbo[:, :], bo_rows[:, :], tgates[:, 0:1], None, ALU.mult).then_inc(gbo_ready, 1)
            dve.wait_ge(rstd1_ready, 1)

            def rows(buf, t):
                return buf[:, t, :] if isinstance(t, int) else buf[:, bass.ds(t, 1), :].squeeze(1)

            def normalise1(t, p):
                if past(t, 2):
                    dve.wait_ge(xk_done, t - 1)
                col = slice(t, t + 1) if isinstance(t, int) else bass.ds(t, 1)
                nc.vector.tensor_scalar(xh[:, p, :], rows(x_all, t), mv1[:, col, 0], rstd1[:, col],
                                        ALU.subtract, ALU.mult).then_inc(xh_ready, 1)

            def scores_max(t, p, h):
                dve.wait_ge(scores_done, 2 * t + h + 1)
                nc.vector.tensor_reduce(s_max[:, p, HH * h:HH * h + HH],
                                        ps[p][:, h, :].rearrange("p (h k) -> p h k", k=S),
                                        AX.X, ALU.max).then_inc(max_ready, 1)

            def scores_sub(t, p, h):
                dve.wait_ge(max_ready, 2 * t + h + 1)
                if past(t, 2):
                    dve.wait_ge(probs_ready, 2 * (t - 2) + h + 1)
                nc.vector.tensor_tensor(s_sub[:, p, HH * h:HH * h + HH, :],
                                        ps[p][:, h, :].rearrange("p (h k) -> p h k", k=S),
                                        s_max[:, p, HH * h:HH * h + HH].unsqueeze(2).broadcast_to([P, HH, S]),
                                        ALU.subtract).then_inc(sub_ready, 1)

            def values(t, p, h2):
                r = slice(64 * h2, 64 * h2 + 64)
                nc.vector.tensor_copy(v_blk[r, p, :, :, HD * h2:HD * h2 + HD],
                                      f_v[r, :].rearrange("p (b n d) -> p b n d", b=2, d=HD)).then_inc(v_ready, 1)

            def step(s, par=None):
                if live(s, 1):
                    normalise1(*at(s, par, 1))
                if live(s, 0):
                    t, p = at(s, par, 0)
                    scores_max(t, p, 0)
                if live(s, -2):
                    t, p = at(s, par, -2)
                    dve.wait_ge(o_turned, t + 1)
                    o_ps = ps_back[:, 0:256].rearrange("p (n c) -> p n c", c=32)
                    nc.vector.reciprocal(o_inv[:, :, :], o_ps[:, :, 16:18]).then_inc(o_inv_ready, 1)
                    dve.wait_ge(o_inv_ready, t + 1)
                    nc.vector.tensor_tensor(o_tok[:, :, :, :],
                                            o_ps[:, :, 0:16].rearrange("p n (h d) -> p n h d", h=2),
                                            o_inv[:, :, :].unsqueeze(3).broadcast_to([P, HP, 2, HD]),
                                            ALU.mult).then_inc(o_tok_ready, 1)
                if live(s, 0):
                    t, p = at(s, par, 0)
                    scores_sub(t, p, 0)
                    scores_max(t, p, 1)
                if live(s, 1):
                    t, p = at(s, par, 1)
                    dve.wait_ge(xT_ready, t + 1)
                    if past(t, 1):
                        dve.wait_ge(k_exp_ready, t)
                    nc.vector.tensor_tensor(kT[:, :, :], f_kT.rearrange("p (a k) -> p a k", a=2),
                                            rows(keep, t).unsqueeze(1).broadcast_to([P, 2, S]),
                                            ALU.mult).then_inc(kT_ready, 1)
                if live(s, 0):
                    t, p = at(s, par, 0)
                    dve.wait_ge(v_done, t + 1)
                    if past(t, 2):
                        dve.wait_ge(pv_done, t - 1)
                    else:
                        dve.wait_ge(zeroed, 6)
                    values(t, p, 0)
                if live(s, -2):
                    t, p = at(s, par, -2)
                    dve.wait_ge(wo_done, t + 1)
                    dve.wait_ge(xbo_ready, t + 1)
                    nc.vector.scalar_tensor_tensor(out=rows(x1_all, t), in0=ps_back[:, 384:512], scalar=tgates[:, 0:1],
                                                   in1=rows(x1_all, t), op0=ALU.mult, op1=ALU.add).then_inc(x1_ready, 1)
                    dve.wait_ge(x1_ready, t + 1)
                if live(s, 0):
                    values(*at(s, par, 0), 1)
                if live(s, -2):
                    t, p = at(s, par, -2)
                    nc.vector.bn_stats(stats2[:, :], rows(x1_all, t)).then_inc(st2_ready, 1)
                    dve.wait_ge(st2_ready, t + 1)
                if live(s, 0):
                    scores_sub(*at(s, par, 0), 1)
                if live(s, -2):
                    t, p = at(s, par, -2)
                    nc.vector.bn_aggr(mv2[:, p, :], stats2[:, :]).then_inc(mv2_ready, 1)
                    dve.wait_ge(mv2_ready, t + 1)
                    nc.vector.tensor_scalar(var2[:, p:p + 1], mv2[:, p, 1:2], LN_EPS, None, ALU.add).then_inc(var2_ready, 1)
                    dve.wait_ge(rstd2_ready, t + 1)
                    if past(t, 2):
                        dve.wait_ge(x2_turned, t - 1)
                    nc.vector.tensor_scalar(xh2[:, p, :], rows(x1_all, t), mv2[:, p, 0:1], rstd2[:, p:p + 1],
                                            ALU.subtract, ALU.mult).then_inc(xh2_ready, 1)

            pipeline(dve, step)

            dve.wait_ge(ld_moe, 16 * 4)
            nc.vector.tensor_copy(wg_hi[:, :], wg_f[:, :]).then_inc(whi_ready, 1)
            nc.vector.tensor_copy(wu_hi[:, :], wu_f[:, :]).then_inc(whi_ready, 1)
            nc.vector.tensor_copy(expert_rows[:, :, :], expert_rows_f[:, :, :]).then_inc(whi_ready, 1)
            dve.wait_ge(whi_ready, 2)
            nc.vector.tensor_tensor(wg_lo[:, :], wg_f[:, :], wg_hi[:, :].bitcast(F32), ALU.subtract).then_inc(wlo_ready, 1)
            nc.vector.tensor_tensor(wu_lo[:, :], wu_f[:, :], wu_hi[:, :].bitcast(F32), ALU.subtract).then_inc(wlo_ready, 1)
            link(nc.vector.memset(combT[:, :].bitcast(F32), 0.0))

            dve.wait_ge(elog_ready, NT)
            link(nc.vector.tensor_scalar(r_den[:, :, :], exp_logit[:, :, :], 1.0, None, ALU.add))
            link(nc.vector.reciprocal(score[:, :, :], r_den[:, :, :]))
            link(nc.vector.tensor_tensor(choice[:, :, :], score[:, :, :],
                                         rbias[:, :].unsqueeze(1).broadcast_to([P, NT, E]), ALU.add))
            quad = choice[:, :, :].rearrange("p t (g a c) -> p (t g) a c", a=2, c=2)
            nc.vector.tensor_tensor(pair_hi[:, :, :], quad[:, :, :, 0], quad[:, :, :, 1], ALU.max)
            link(nc.vector.tensor_tensor(pair_lo[:, :, :], quad[:, :, :, 0], quad[:, :, :, 1], ALU.min))
            nc.vector.tensor_tensor(top1[:, :], pair_hi[:, :, 0], pair_hi[:, :, 1], ALU.max)
            nc.vector.tensor_tensor(low_hi[:, :], pair_hi[:, :, 0], pair_hi[:, :, 1], ALU.min)
            link(nc.vector.tensor_tensor(hi_low[:, :], pair_lo[:, :, 0], pair_lo[:, :, 1], ALU.max))
            link(nc.vector.tensor_tensor(top2[:, :], low_hi[:, :], hi_low[:, :], ALU.max))
            link(nc.vector.tensor_tensor(g_score[:, :, :].rearrange("p t g -> p (t g)"), top1[:, :], top2[:, :], ALU.add))
            other = g_score[:, :, :].unsqueeze(2).broadcast_to([P, NT, GROUPS, GROUPS])
            own = g_score[:, :, :].unsqueeze(3).broadcast_to([P, NT, GROUPS, GROUPS])
            nc.vector.tensor_tensor(g_ge[:, :, :, :], other, own, ALU.is_ge)
            link(nc.vector.tensor_tensor(g_gt[:, :, :, :], other, own, ALU.is_gt))
            for k, g_cmp in enumerate((g_ge, g_gt)):
                last = nc.vector.tensor_tensor(g_cmp[:, :, :, :], g_cmp[:, :, :, :],
                                               group_order[:, k, :, :].unsqueeze(1).broadcast_to([P, NT, GROUPS, GROUPS]),
                                               ALU.mult)
            link(last)
            link(nc.vector.tensor_tensor(g_ge[:, :, :, :], g_ge[:, :, :, :], g_gt[:, :, :, :], ALU.add))
            link(nc.vector.tensor_reduce(g_rank[:, :, :], g_ge[:, :, :, :], AX.X, ALU.add))
            link(nc.vector.tensor_scalar(g_keep[:, :, :], g_rank[:, :, :], 1.5, None, ALU.is_lt))
            link(nc.vector.tensor_scalar(g_neg[:, :, :], g_keep[:, :, :], -1.0, -NEG, ALU.add, ALU.mult))
            grouped = [v[:, :, :].rearrange("p t (g e) -> p (t g) e", g=GROUPS) for v in (choice, masked)]
            per_group = [v[:, :, :].rearrange("p t g -> p (t g)").unsqueeze(2).broadcast_to([P, NT * GROUPS, PER_GROUP])
                         for v in (g_keep, g_neg)]
            link(nc.vector.tensor_tensor(grouped[1], grouped[0], per_group[0], ALU.mult))
            link(nc.vector.tensor_tensor(grouped[1], grouped[1], per_group[1], ALU.add))
            for t in range(NT):
                last = nc.vector.max(best[:, t, :], masked[:, t, :])
            link(last)
            link(nc.vector.memset(best[:, :, TOP_K:8], 3.0e38))
            for t in range(NT):
                last = nc.vector.match_replace(rest[:, t, :], best[:, t, :], masked[:, t, :], -3.0e38)
            link(last)
            link(nc.vector.tensor_tensor(chosen[:, :, :], rest[:, :, :], masked[:, :, :], ALU.not_equal))
            link(nc.vector.tensor_tensor(w_sel[:, :, :], score[:, :, :], chosen[:, :, :], ALU.mult))
            link(nc.vector.tensor_reduce(w_sum[:, :], w_sel[:, :, :], AX.X, ALU.add))
            link(nc.vector.tensor_scalar(w_sum[:, :], w_sum[:, :], 1e-20, None, ALU.add))
            link(nc.vector.reciprocal(w_inv[:, :], w_sum[:, :]))
            link(nc.vector.tensor_tensor(comb[:, :, :], w_sel[:, :, :],
                                         w_inv[:, :].unsqueeze(2).broadcast_to([P, NT, E]), ALU.mult))
            link(nc.vector.tensor_scalar(comb[:, :, :], comb[:, :, :], ROUTED_SCALE, None, ALU.mult))
            link(nc.vector.tensor_copy(comb_hi[:, :, :], comb[:, :, :]))
            nc.vector.tensor_copy(comb_parts[:, :, 0, :], comb_hi[:, :, :].bitcast(F32)).then_inc(parts_ready, 1)
            nc.vector.tensor_tensor(comb_parts[:, :, 1, :], comb[:, :, :], comb_hi[:, :, :].bitcast(F32),
                                    ALU.subtract).then_inc(parts_ready, 1)

            def finish(g):
                dve.wait_ge(down_done, EP * (g + 1))
                tiles = bass.ds(GT * g, GT)
                nc.vector.scalar_tensor_tensor(out=y_out[:, tiles, :].rearrange("p t d -> p (t d)"), in0=ps_y[:, :],
                                               scalar=tgates[:, 1:2],
                                               in1=x1_all[:, tiles, :].rearrange("p t d -> p (t d)"),
                                               op0=ALU.mult, op1=ALU.add).then_inc(y_ready, 1)

            def pair(g, q):
                n = EP * g + q
                dve.wait_ge(silu_ready, n + 1)
                dve.wait_ge(up_done, n + 1)
                if past(n, 2):
                    dve.wait_ge(hid_ready, n - 1)
                nc.vector.tensor_tensor(gu[:, q % 2, :], silu_g[:, q % 2, :], ps_up[q % 2], ALU.mult).then_inc(gu_ready, 1)
                dve.wait_ge(gu_ready, n + 1)
                dve.wait_ge(comb_done, n + 1)
                if past(n, 2):
                    dve.wait_ge(down_done, n - 1)
                nc.vector.tensor_tensor(hid[:, q % 2, :], gu[:, q % 2, :], ps_comb[q % 2], ALU.mult).then_inc(hid_ready, 1)

            for q in range(EP):
                pair(0, q)
            with dve.Fori(1, NG) as g:
                for q in range(EP):
                    pair(g, q)
                    if q == 1:
                        finish(g - 1)
            finish(NG - 1)

        @block.tensor
        def _(pe):
            def turn(dst, src):
                return nc.tensor.transpose(dst, src, ident[:, :])

            pe.wait_ge(ld_front, 16 * 5)

            def front(t, p):
                pe.wait_ge(xh_ready, t + 1)
                if past(t, 1):
                    pe.wait_ge(q_ready, 2 * t)
                turn(f_xT, xh[:, p, :])
                pe.wait_ge(ld_ctx[p], 16 * ctx_loads(t))
                for half in range(2):
                    for b in range(2):
                        last = nc.tensor.matmul(f_kT[64 * b:64 * b + 64, 64 * half:64 * half + 64],
                                                wk[:, 64 * half:64 * half + 64], ctxT[:, p, 64 * b:64 * b + 64],
                                                start=True, stop=True)
                last.then_inc(xk_done, 1)

            def values(t, p):
                pe.wait_ge(q_ready, 2 * t + 2)
                for b in range(2):
                    for h2 in range(2):
                        last = nc.tensor.matmul(f_v[64 * h2:64 * h2 + 64, 64 * b:64 * b + 64],
                                                ctxT[:, p, 64 * b:64 * b + 64], v_pair(wv, h2),
                                                start=True, stop=True)
                last.then_inc(v_done, 1)

            loads = {}

            def ctx_loads(t):
                return t // 2 + 1 if isinstance(t, int) else loads["here"]

            def scores(t, p, h):
                if h == 0:
                    pe.wait_ge(q_ready, 2 * t + 2)
                    pe.wait_ge(k_exp_ready, t + 1)
                    if not past(t, 1):
                        pe.wait_ge(batch_rows_ready, 1)
                        pe.wait_ge(neg_ready, 1)
                if past(t, 2):
                    pe.wait_ge(sub_ready, 2 * (t - 2) + h + 1)
                row = slice(t, t + 1) if isinstance(t, int) else bass.ds(t, 1)
                nc.tensor.matmul(ps[p][:, h, :], batch_rows[:, :],
                                 neg_rows[:, row, :].broadcast_to([P, HH, S]), start=True, stop=False)
                nc.tensor.matmul(ps[p][:, h, :], q_blk[:, p, h, :],
                                 k_exp[:, p, h, :, :].rearrange("p h k -> p (h k)"),
                                 start=False, stop=True).then_inc(scores_done, 1)

            def turn_probs(t, p, h):
                pe.wait_ge(probs_ready, 2 * t + h + 1)
                if past(t, 1):
                    pe.wait_ge(pT_ready, 2 * (t - 1) + h + 1)
                for n in range(4):
                    c = 4 * h + n
                    last = turn(ps_pT[h][:, n, :], probs[:, p, P * c:P * c + P])
                last.then_inc(pT_done, 1)

            def step(s, par=None):
                if live(s, 0):
                    scores(*at(s, par, 0), 0)
                if live(s, -2):
                    t, p = at(s, par, -2)
                    pe.wait_ge(oT_ready, t + 1)
                    turn(ps_back[:, 0:128], oT[:, 0, :])
                    turn(ps_back[:, 128:256], oT[:, 1, :]).then_inc(o_turned, 1)
                if live(s, 0):
                    scores(*at(s, par, 0), 1)
                if live(s, 0):
                    values(*at(s, par, 0))
                if live(s, 1):
                    front(*at(s, par, 1))
                if live(s, -2):
                    t, p = at(s, par, -2)
                    pe.wait_ge(o_tok_ready, t + 1)
                    turn(ps_back[:, 256:384], o_tok[:, :, :, :].rearrange("p n h d -> p (n h d)")).then_inc(on_turned, 1)
                if live(s, -1):
                    turn_probs(*at(s, par, -1), 0)
                if live(s, -2):
                    t, p = at(s, par, -2)
                    pe.wait_ge(onT_ready, t + 1)
                    if not past(t, 1):
                        pe.wait_ge(ld_back, 16 * 7)
                    nc.tensor.matmul(ps_back[:, 384:512], onT[:, :], wo[:, :], start=True, stop=True).then_inc(wo_done, 1)
                if live(s, 1):
                    t, p = at(s, par, 1)
                    pe.wait_ge(xT_ready, t + 1)
                    pe.wait_ge(kT_ready, t + 1)
                    if live(s, 0):
                        pe.wait_ge(v_ready, 2 * t)
                    for half in range(2):
                        for b in range(2):
                            last = nc.tensor.matmul(f_qT[64 * b:64 * b + 64, 64 * half:64 * half + 64],
                                                    wq[:, 64 * half:64 * half + 64], xT[:, 64 * b:64 * b + 64],
                                                    start=True, stop=True)
                    last.then_inc(q_done, 1)
                if live(s, -1):
                    turn_probs(*at(s, par, -1), 1)
                if live(s, -3):
                    t, p = at(s, par, -3)
                    pe.wait_ge(xh2_ready, t + 1)
                    if live(s, -2):
                        pe.wait_ge(x1_ready, t + 2)
                    else:
                        pe.wait_ge(elog_ready, t)
                    if past(t, 1):
                        pe.wait_ge(x2lo_ready, t)
                    turn(ps_back[:, 0:128], xh2[:, p, :]).then_inc(x2_turned, 1)
                    pe.wait_ge(x2T_ready, t + 1)
                    nc.tensor.matmul(ps_back[:, 128:128 + E], x2T[:, :], rwT[:, :], start=True, stop=True
                                     ).then_inc(logits_done, 1)
                if live(s, -1):
                    t, p = at(s, par, -1)
                    pe.wait_ge(pT_ready, 2 * t + 2)
                    if live(s, -3):
                        pe.wait_ge(elog_ready, t - 1)
                    elif live(s, -2):
                        pe.wait_ge(x1_ready, t)
                    for n in range(HP):
                        for b in range(2):
                            r = 32 * (n % 4)
                            c = P * (n // 4) + 64 * b
                            last = nc.tensor.matmul(ps_back[r:r + 32, c:c + 64], v_blk[:, p, b, n, :],
                                                    pT[:, n, 64 * b:64 * b + 64], start=True, stop=True)
                    last.then_inc(pv_done, 1)

            for s in range(-1, FIRST_STEP):
                step(s)
            with pe.Fori(0, (NT - 1 - FIRST_STEP) // 2) as i:
                loads["here"] = i + (FIRST_STEP + 3) // 2
                for u in range(2):
                    step(2 * i + (FIRST_STEP + u), 1 - u)
            for s in range(NT - 1, NT + 3):
                step(s)

            pe.wait_ge(parts_ready, 2)
            pe.wait_ge(x2lo_ready, NT)
            for g in range(NG):
                for k in range(GT):
                    last = nc.tensor.transpose((ps_gate + ps_up)[g][0:2 * E, P * k:P * k + P],
                                               comb_parts[:, GT * g + k, :, :].rearrange("p a e -> p (a e)"), ident[:, :])
                last.then_inc(parts_turned, 1)

            pe.wait_ge(whi_ready, 3)
            pe.wait_ge(wlo_ready, 2)
            pe.wait_ge(combT_ready, NG)

            def product3(dst, w_hi, w_lo, c, tok, done):
                w = slice(P * c, P * c + P)
                nc.tensor.matmul(dst, w_lo[:, w], x2_hi[:, tok], start=True, stop=False)
                nc.tensor.matmul(dst, w_hi[:, w], x2_lo[:, tok], start=False, stop=False)
                nc.tensor.matmul(dst, w_hi[:, w], x2_hi[:, tok], start=False, stop=True).then_inc(done, 1)

            def gate_up(g, q):
                n = EP * g + q
                early = isinstance(n, int) and n < 2
                tok = bass.ds(GN * g, GN)
                if not early:
                    pe.wait_ge(silu_ready, n - 1)
                product3(ps_gate[q % 2], wg_hi, wg_lo, q, tok, gate_done)
                if not early:
                    pe.wait_ge(gu_ready, n - 1)
                product3(ps_up[q % 2], wu_hi, wu_lo, q, tok, up_done)
                if not early:
                    pe.wait_ge(hid_ready, n - 1)
                nc.tensor.matmul(ps_comb[q % 2], expert_rows[:, q, :], combT[:, tok], start=True, stop=True
                                 ).then_inc(comb_done, 1)

            def down(g, q, first=False):
                n = EP * g + q
                pe.wait_ge(hid_ready, n + 1)
                if q == 0 and not first:
                    pe.wait_ge(y_ready, g)
                for k in range(GT):
                    last = nc.tensor.matmul(ps_y[:, P * k:P * k + P], hid[:, q % 2, P * k:P * k + P], wd[:, q, :],
                                            start=(q == 0 and k == 0), stop=(q == EP - 1), skip_group_check=True)
                last.then_inc(down_done, 1)

            gate_up(0, 0)
            for q in range(1, EP):
                gate_up(0, q)
                down(0, q - 1, True)
            with pe.Fori(1, NG) as g:
                gate_up(g, 0)
                down(g - 1, EP - 1)
                for q in range(1, EP):
                    gate_up(g, q)
                    down(g, q - 1)
            down(NG - 1, EP - 1)


def kernel(**inputs):
    import concourse.bacc as _bacc
    from concourse.bass_utils import run_bass_kernel_spmd as _run

    f = {k: np.asarray(v) for k, v in inputs.items()}
    arrays = {
        "x": f["x"],
        "ctxT": f["ctx_1024"].reshape(B * S, D).T,
        "itok": f["itok_BxS2_0_99"],
        "g_xattn": f["g_xattn"],
        "g_ffn": f["g_ffn"],
        "wq": f["L0_xattn_Wq"],
        "wk": f["L0_xattn_Wk"],
        "wv": f["L0_xattn_Wv"],
        "wo": f["L0_xattn_Wo"],
        "bo": f["L0_xattn_bo"],
        "rwT": f["L0_ffn_router_weight"].T,
        "rbias": f["L0_ffn_router_bias"],
        "wgT": f["L0_ffn_w_gate"].reshape(E * I, D).T,
        "wuT": f["L0_ffn_w_up"].reshape(E * I, D).T,
        "wdT": f["L0_ffn_w_down"].transpose(0, 2, 1).reshape(E * I, D),
    }
    arrays.update(constants())
    arrays = {k: np.ascontiguousarray(v) for k, v in arrays.items()}
    nc = _bacc.Bacc("TRN2", target_bir_lowering=False, num_devices=1)
    aps = {k: nc.dram_tensor(f"in_{k}", v.shape, mybir.dt.from_np(v.dtype), kind="ExternalInput").ap()
           for k, v in arrays.items()}
    out = nc.dram_tensor("out_x", (B, S, D), F32, kind="ExternalOutput").ap()
    build(nc, aps, out)
    r = _run(nc, [{f"in_{k}": v for k, v in arrays.items()}], core_ids=[0])
    return r.results[0]["out_x"]
```

```python
from contextlib import ExitStack

import numpy as np

import concourse.bass as bass
from concourse import mybir

F32 = mybir.dt.float32
F32R = mybir.dt.float32r
BF16 = mybir.dt.bfloat16
I32 = mybir.dt.int32
ALU = mybir.AluOpType
ACT = mybir.ActivationFunctionType
AX = mybir.AxisListType

P = 128
B, S, D = 32, 64, 128
H, HD = 16, 8
E, I = 16, 64
NT = B * S // P
HH = H // 2
HP = H // 2
EP = E // 2
GT = 4
NG = NT // GT
NU = NT // 2
UN = 2 * P
ROUTE_STEPS = 39
LOOP_FROM, LOOP_TO = 3, NU - 2
GN = GT * P
NEG = -1000000000.0
NPIECE = 3
X_CHUNKS = [(0, 2), (2, 4), (4, 10), (10, NT)]
LN_EPS = 1e-5
SM_SCALE = float(1.0 / np.sqrt(HD))
GROUPS, PER_GROUP, TOP_K = 4, 4, 4
FILL = 6
ROUTED_SCALE = 2.5


def neg_pieces():
    rest, out = np.float32(NEG), []
    for _ in range(NPIECE):
        piece = (rest.reshape(1).view(np.uint32) & np.uint32(0xFFFF0000)).view(np.float32)[0]
        out.append(piece)
        rest = np.float32(rest - piece)
    assert rest == 0
    return out


def constants():
    ident = np.eye(P, dtype=np.float32)
    p = np.arange(P)
    head_mask = ((p[:, None] % 64) // HD == np.arange(HH)[None, :]).astype(np.float32)
    batch_rows = np.zeros((P, P), np.float32)
    neg_col = np.zeros((P, 1), np.float32)
    for b in range(2):
        for i, v in enumerate(neg_pieces()):
            batch_rows[64 * b + i, 64 * b:64 * b + 64] = 1.0
            neg_col[64 * b + i] = v
    expert_rows = np.zeros((P, EP, P), np.float32)
    for q in range(EP):
        for j in range(2):
            for part in range(2):
                expert_rows[16 * part + 2 * q + j, q, 64 * j:64 * j + 64] = 1.0
    g, j = np.arange(GROUPS)[:, None], np.arange(GROUPS)[None, :]
    before = np.broadcast_to((j < g).astype(np.float32), (P, GROUPS, GROUPS))
    after = np.broadcast_to((j > g).astype(np.float32), (P, GROUPS, GROUPS))
    order = np.stack([before, after], 1).reshape(P, -1)
    return {"c_tables": np.concatenate([ident, head_mask, neg_col, batch_rows, order], 1),
            "c_expert_rows": expert_rows.reshape(P, EP * P)}


def build(nc, a, out):
    ctx = ExitStack()
    with ctx:
        def sb(name, shape, dt=F32):
            return ctx.enter_context(nc.sbuf_tensor(name, shape, dt))

        def sem(name):
            return ctx.enter_context(nc.semaphore(name))

        def split(buf, widths):
            ends = np.cumsum(widths).tolist()
            return [buf[:, e - w:e] for e, w in zip(ends, widths)]

        tables = sb("tables", [P, P + HH + 1 + P + 2 * GROUPS * GROUPS])
        ident, head_mask, neg_col, batch_rows_f, group_order = split(
            tables, [P, HH, 1, P, 2 * GROUPS * GROUPS])
        group_order = group_order.rearrange("p (o g j) -> p o g j", o=2, g=GROUPS)
        batch_rows = sb("batch_rows", [P, P], BF16)
        wk = sb("wk", [P, P])
        w_qv = sb("w_qv", [P, 2 * P])
        wq, wv = split(w_qv, [P, P])
        w_back = sb("w_back", [P, P + E])
        wo, rwT = split(w_back, [P, E])
        rows = sb("rows", [P, P + E + 2])
        bo_rows, rbias, gates = split(rows, [P, E, 2])
        tgates = sb("tgates", [P, 2])
        gbo = sb("gbo", [P, P])
        expert_rows_f = sb("expert_rows_f", [P, EP, P])
        expert_rows = sb("expert_rows", [P, EP, P], F32R)
        wg_f = sb("wg_f", [P, E * I])
        wu_f = sb("wu_f", [P, E * I])
        wg_hi = sb("wg_hi", [P, E * I], F32R)
        wg_lo = sb("wg_lo", [P, E * I], F32R)
        wu_hi = sb("wu_hi", [P, E * I], F32R)
        wu_lo = sb("wu_lo", [P, E * I], F32R)
        wd = sb("wd", [P, EP, D])

        x_all = sb("x_all", [P, NT, D])
        x1_all = sb("x1_all", [P, NT, D])
        stats = sb("stats", [P, NT, 6])
        mv1 = sb("mv1", [P, NT, 2])
        var1 = sb("var1", [P, NT])
        rstd1 = sb("rstd1", [P, NT])
        minus_half = sb("minus_half", [P, NT])
        keys_tok = sb("keys_tok", [P, NT, S], I32)
        keep = sb("keep", [P, NT, S])
        neg_rows = sb("neg_rows", [P, NT, S], BF16)
        ctx_k = sb("ctx_k", [P, 2, P])
        ctx_v = sb("ctx_v", [P, 2, P])
        xh = sb("xh", [P, 2, D])
        xT = sb("xT", [P, UN])
        q_blk = sb("q_blk", [P, 2, 2, P])
        kT = sb("kT", [P, 2, 2, S])
        k_exp = sb("k_exp", [P, 2, 2, HH, S])
        v_blk = sb("v_blk", [P, 4, HP, 32])
        s_max = sb("s_max", [P, 2, H])
        s_sub = sb("s_sub", [P, 2, H, S])
        probs = sb("probs", [P, 2, H * S])
        pT = sb("pT", [P, 2, HP, P])
        oT = sb("oT", [P, 4, P])
        o_inv = sb("o_inv", [P, 2 * HP, 2])
        o_tok = sb("o_tok", [P, 2 * HP, 2, HD])
        onT = sb("onT", [P, 2, P])
        stats2 = sb("stats2", [P, 2, 6])
        mv2 = sb("mv2", [P, 2, 2])
        var2 = sb("var2", [P, 2])
        rstd2 = sb("rstd2", [P, 2])
        xh2 = sb("xh2", [P, 2, D])
        x2T = sb("x2T", [P, UN])
        x2_hi = sb("x2_hi", [P, NT * P], F32R)
        x2_lo = sb("x2_lo", [P, NT * P], F32R)

        exp_logit = sb("exp_logit", [P, NT, E])
        r_den = sb("r_den", [P, GT, E])
        score = sb("score", [P, GT, E])
        choice = sb("choice", [P, GT, E])
        pair_hi = sb("pair_hi", [P, GT * GROUPS, 2])
        pair_lo = sb("pair_lo", [P, GT * GROUPS, 2])
        top1 = sb("top1", [P, GT * GROUPS])
        low_hi = sb("low_hi", [P, GT * GROUPS])
        hi_low = sb("hi_low", [P, GT * GROUPS])
        top2 = sb("top2", [P, GT * GROUPS])
        g_score = sb("g_score", [P, GT, GROUPS])
        g_ge = sb("g_ge", [P, GT, GROUPS, GROUPS])
        g_gt = sb("g_gt", [P, GT, GROUPS, GROUPS])
        g_rank = sb("g_rank", [P, GT, GROUPS])
        g_keep = sb("g_keep", [P, GT, GROUPS])
        g_neg = sb("g_neg", [P, GT, GROUPS])
        masked = sb("masked", [P, GT, E])
        best = sb("best", [P, GT, 8])
        rest = sb("rest", [P, GT, E])
        chosen = sb("chosen", [P, GT, E])
        w_sel = sb("w_sel", [P, GT, E])
        w_sum = sb("w_sum", [P, GT])
        w_inv = sb("w_inv", [P, GT])
        comb = sb("comb", [P, GT, E])
        comb_hi = sb("comb_hi", [P, GT, E], F32R)
        comb_parts = sb("comb_parts", [P, GT, 2, E])
        combT = sb("combT", [P, NG * GN], F32R)

        silu_g = sb("silu_g", [P, 2, GN])
        gu = sb("gu", [P, 2, GN])
        hid = sb("hid", [P, 4, GN])
        y_out = sb("y_out", [P, NT, D])

        ps = [ctx.enter_context(nc.psum_tensor(f"ps_scores{i}", [P, 2, 512], F32)) for i in range(2)]
        ps_pT = [ctx.enter_context(nc.psum_tensor(f"ps_pT{i}", [P, 4, P], F32)) for i in range(2)]
        ps_front = ctx.enter_context(nc.psum_tensor("ps_front", [P, 512], F32))
        ps_back = ctx.enter_context(nc.psum_tensor("ps_back", [P, 512], F32))
        f_xT, f_kT = ps_front[:, 0:UN], ps_front[:, UN:2 * UN]
        f_v, f_qT = ps_front[:, 0:UN], ps_front[:, UN:2 * UN]
        ps_gate = [ps[0][:, 0, :], ps[0][:, 1, :]]
        ps_up = [ps[1][:, 0, :], ps[1][:, 1, :]]
        ps_comb = [ps_pT[0][:, :, :].rearrange("p a b -> p (a b)"), ps_pT[1][:, :, :].rearrange("p a b -> p (a b)")]
        ps_y = ps_front

        ld_tables, ld_wk, ld_w, ld_mask, ld_rows, ld_back = (
            sem("ld_tables"), sem("ld_wk"), sem("ld_w"), sem("ld_mask"), sem("ld_rows"), sem("ld_back"))
        ld_moe, ld_wd = sem("ld_moe"), sem("ld_wd")
        ld_x = [sem(f"ld_x{c}") for c in range(len(X_CHUNKS))]
        ld_ctx_k, ld_ctx_v = sem("ld_ctx_k"), sem("ld_ctx_v")
        half_set, q_zeroed, v_set, combT_zeroed = sem("half_set"), sem("q_zeroed"), sem("v_set"), sem("combT_zeroed")
        chain = sem("chain")
        var1_ready, rstd1_ready = sem("var1_ready"), sem("rstd1_ready")
        keep_ready, batch_rows_ready, neg_ready, tanh_ready, gbo_ready = (
            sem("keep_ready"), sem("batch_rows_ready"), sem("neg_ready"), sem("tanh_ready"), sem("gbo_ready"))
        xh_ready, xk_done, xT_ready, kT_ready, k_exp_ready, first_k_exp = (
            sem("xh_ready"), sem("xk_done"), sem("xT_ready"), sem("kT_ready"), sem("k_exp_ready"), sem("first_k_exp"))
        qv_done, q_ready, v_ready, xbo_ready = sem("qv_done"), sem("q_ready"), sem("v_ready"), sem("xbo_ready")
        scores_done, max_ready, sub_ready, probs_ready = (
            sem("scores_done"), sem("max_ready"), sem("sub_ready"), sem("probs_ready"))
        pT_done, pT_ready = sem("pT_done"), sem("pT_ready")
        pv_done, oT_ready, o_turned, o_inv_ready, o_tok_ready = (
            sem("pv_done"), sem("oT_ready"), sem("o_turned"), sem("o_inv_ready"), sem("o_tok_ready"))
        on_turned, onT_ready, wo_done, x1_ready = sem("on_turned"), sem("onT_ready"), sem("wo_done"), sem("x1_ready")
        st2_ready, mv2_ready, var2_ready, rstd2_ready, xh2_ready = (
            sem("st2_ready"), sem("mv2_ready"), sem("var2_ready"), sem("rstd2_ready"), sem("xh2_ready"))
        x2_turned, x2T_ready, x2hi_ready, x2lo_ready, logits_done, elog_ready = (
            sem("x2_turned"), sem("x2T_ready"), sem("x2hi_ready"), sem("x2lo_ready"), sem("logits_done"), sem("elog_ready"))
        whi_ready, wlo_ready = sem("whi_ready"), sem("wlo_ready")
        parts_ready, parts_turned, combT_ready = sem("parts_ready"), sem("parts_turned"), sem("combT_ready")
        gate_done, up_done, comb_done, silu_ready, gu_ready, hid_ready, down_done = (
            sem("gate_done"), sem("up_done"), sem("comb_done"), sem("silu_ready"), sem("gu_ready"),
            sem("hid_ready"), sem("down_done"))
        y_ready, y_sent = sem("y_ready"), sem("y_sent")
        route_step = sem("route_step")

        x_dram = a["x"].rearrange("b s d -> (b s) d").rearrange("(t p) d -> p t d", p=P)
        out_dram = out.rearrange("b s d -> (b s) d").rearrange("(t p) d -> p t d", p=P)
        ctx_dram = a["ctxT"]

        def v_pair(w, h2):
            return w[:, :].rearrange("p (n h d) -> p n h d", h=2, d=HD)[:, :, h2, :]

        block = ctx.enter_context(nc.Block())

        def pipeline(eng, step):
            for u in range(-1, LOOP_FROM):
                step(u)
            with eng.Fori(LOOP_FROM, LOOP_TO) as u:
                step(u)
            for u in range(LOOP_TO, NU + 3):
                step(u)

        def live(u, d):
            return not isinstance(u, int) or 0 <= u + d < NU

        def step_is(u, k):
            return isinstance(u, int) and u == k

        def past(t, k):
            return not isinstance(t, int) or t >= k

        def unit_tiles(u):
            return bass.ds(2 * u, 2)

        def tile_of(buf, u, j):
            return buf[:, bass.ds(2 * u + j, 1), :].squeeze(1)

        def flat(ap):
            return ap.rearrange("p t d -> p (t d)")

        @block.sync
        def _(sp):
            def load_x(c):
                a_, b_ = X_CHUNKS[c]
                sp.dma_start(x_all[:, a_:b_, :], x_dram[:, a_:b_, :]).then_inc(ld_x[c], 16)

            load_x(0)

            def unit_ctx(u):
                return ctx_dram[:, bass.ds(UN * u, UN)].rearrange("d (t p) -> d t p", t=2)

            def step(u):
                if live(u, 1):
                    if past(u, 0):
                        sp.wait_ge(xk_done, u + 1)
                    sp.dma_start(ctx_k[:, :, :], unit_ctx(u + 1)).then_inc(ld_ctx_k, 16)
                if step_is(u, -1):
                    sp.dma_start(tables[:, :], a["c_tables"]).then_inc(ld_tables, 16)
                    for c in range(1, len(X_CHUNKS)):
                        load_x(c)
                    sp.dma_start(w_back[:, :], a["w_back"]).then_inc(ld_back, 16)
                if step_is(u, 0):
                    sp.dma_start(wg_f[:, :], a["wgT"]).then_inc(ld_moe, 16)
                    sp.dma_start(wu_f[:, :], a["wuT"]).then_inc(ld_moe, 16)
                    sp.dma_start(expert_rows_f[:, :, :], a["c_expert_rows"].rearrange("p (q c) -> p q c", q=EP)
                                 ).then_inc(ld_moe, 16)
                    sp.dma_start(wd[:, :, :], a["wdT"].rearrange("(q p) d -> p q d", p=P)).then_inc(ld_wd, 16)
                if live(u, 0):
                    if past(u, 1):
                        sp.wait_ge(qv_done, u + 1)
                    sp.dma_start(ctx_v[:, :, :], unit_ctx(u)).then_inc(ld_ctx_v, 16)

            pipeline(sp, step)
            with sp.Fori(0, NG) as g:
                sp.wait_ge(y_ready, g + 1)
                sp.dma_start(out_dram[:, bass.ds(GT * g, GT), :], y_out[:, bass.ds(GT * g, GT), :]).then_inc(y_sent, 16)
            sp.wait_ge(y_sent, 16 * NG)

        @block.scalar
        def _(act):
            act.dma_start(wk[:, :], a["wk"]).then_inc(ld_wk, 16)
            act.dma_start(w_qv[:, :], a["w_qv"]).then_inc(ld_w, 16)
            for b in range(2):
                act.dma_start(flat(keys_tok[64 * b:64 * b + 64, :, :]), a["itok"][b:b + 1].partition_broadcast(64)
                              ).then_inc(ld_mask, 16)
            act.dma_start(rows[:, :], a["rows"].partition_broadcast(P)).then_inc(ld_rows, 16)

            act.wait_ge(ld_tables, 16)
            nc.scalar.copy(batch_rows[:, :], batch_rows_f[:, :]).then_inc(batch_rows_ready, 1)

            def exp_half(u, j, h):
                n = 4 * u + 2 * j + h + 1
                act.wait_ge(sub_ready, n)
                if past(u, 1):
                    act.wait_ge(pT_done, n - 4)
                nc.scalar.activation(probs[:, j, 512 * h:512 * h + 512],
                                     flat(s_sub[:, j, HH * h:HH * h + HH, :]),
                                     ACT.Exp, scale=SM_SCALE).then_inc(probs_ready, 1)

            def probs_out(u, j, h):
                act.wait_ge(pT_done, 4 * u + 2 * j + h + 1)
                if past(u, 1):
                    act.wait_ge(pv_done, u)
                nc.scalar.copy(pT[:, j, 4 * h:4 * h + 4, :], ps_pT[h][:, :, :]).then_inc(pT_ready, 1)

            def q_out(u, j):
                if past(u, 0):
                    act.wait_ge(scores_done, 4 * u + 2 * j + 2)
                for b in range(2):
                    r = slice(64 * b, 64 * b + 64)
                    nc.scalar.copy(q_blk[r, j, :, 64 * b:64 * b + 64],
                                   f_qT[r, P * j:P * j + P].rearrange("p (a q) -> p a q", a=2)).then_inc(q_ready, 1)

            def step(u):
                if live(u, -1):
                    exp_half(u - 1, 1, 1)
                if live(u, -3):
                    act.wait_ge(logits_done, u - 2)
                    late = step_is(u, NU + 1) or step_is(u, NU + 2)
                    nc.scalar.activation(exp_logit[:, unit_tiles(u - 3), :],
                                         ps_back[:, UN:UN + 2 * E].rearrange("p (t e) -> p t e", t=2),
                                         ACT.Copy if late else ACT.Exp, scale=1.0 if late else -1.0
                                         ).then_inc(elog_ready, 1)
                if live(u, -1):
                    probs_out(u - 1, 1, 0)
                if step_is(u, NU):
                    silu(0, 0)
                if live(u, 0):
                    exp_half(u, 0, 0)
                if live(u, -1):
                    probs_out(u - 1, 1, 1)
                if step_is(u, NU):
                    silu(0, 1)
                if live(u, 0):
                    exp_half(u, 0, 1)
                if live(u, 1):
                    act.wait_ge(xk_done, u + 2)
                    if past(u, 0):
                        act.wait_ge(qv_done, u + 1)
                    nc.scalar.copy(xT[:, :], f_xT).then_inc(xT_ready, 1)
                    if step_is(u, 0):
                        act.wait_ge(ld_moe, 16 * 3)
                        nc.scalar.copy(wg_hi[:, :], wg_f[:, :]).then_inc(whi_ready, 1)
                        nc.scalar.copy(expert_rows[:, :, :], expert_rows_f[:, :, :]).then_inc(whi_ready, 1)
                if live(u, -1):
                    act.wait_ge(pv_done, u)
                    nc.scalar.copy(flat(oT[:, :, :]), ps_back[:, :]).then_inc(oT_ready, 1)
                if step_is(u, NU):
                    act.wait_ge(combT_zeroed, 1)
                    weights_out(0, ps_front)
                    silu(0, 2)
                if live(u, 1):
                    act.wait_ge(qv_done, u + 2)
                    if step_is(u, -1):
                        act.wait_ge(q_zeroed, 1)
                    q_out(u, 0)
                    if step_is(u, 0):
                        nc.scalar.copy(wu_hi[:, :], wu_f[:, :]).then_inc(whi_ready, 1)
                if live(u, -1):
                    act.wait_ge(on_turned, u)
                    nc.scalar.copy(flat(onT[:, :, :]), ps_back[:, 0:UN]).then_inc(onT_ready, 1)
                if step_is(u, NU):
                    silu(0, 3)
                if step_is(u, NU + 1):
                    silu(0, 4)
                if step_is(u, NU + 2):
                    silu(0, 5)
                if live(u, 0):
                    exp_half(u, 1, 0)
                if live(u, 1):
                    if live(u, 0):
                        act.wait_ge(v_ready, 2 * u + 2)
                    q_out(u, 1)
                if live(u, 0):
                    probs_out(u, 0, 0)
                    probs_out(u, 0, 1)
                if live(u, -2):
                    act.wait_ge(x2_turned, u - 1)
                    if live(u, -3):
                        act.wait_ge(logits_done, u - 2)
                        act.wait_ge(x2lo_ready, u - 2)
                    nc.scalar.copy(x2T[:, :], ps_back[:, 0:UN]).then_inc(x2T_ready, 1)
                    act.wait_ge(x2T_ready, u - 1)
                    nc.scalar.copy(x2_hi[:, bass.ds(UN * (u - 2), UN)], x2T[:, :]).then_inc(x2hi_ready, 1)
                if step_is(u, -1):
                    act.wait_ge(ld_rows, 16)
                    nc.scalar.activation(tgates[:, :], gates[:, :], ACT.Tanh).then_inc(tanh_ready, 1)

            def weights_out(g, bank):
                act.wait_ge(parts_turned, g + 1)
                nc.scalar.copy(combT[0:2 * E, bass.ds(GN * g, GN)], bank[0:2 * E, :]).then_inc(combT_ready, 1)

            def silu(g, q):
                n = EP * g + q
                act.wait_ge(gate_done, n + 1)
                if past(n, 2):
                    act.wait_ge(gu_ready, n - 1)
                nc.scalar.activation(silu_g[:, q % 2, :], ps_gate[q % 2], ACT.Silu).then_inc(silu_ready, 1)

            pipeline(act, step)
            for q in range(FILL, EP - 1):
                silu(0, q)
            late_logits = exp_logit[:, NT - GT:NT, :]
            act.wait_ge(elog_ready, NU)
            nc.scalar.activation(late_logits, late_logits, ACT.Exp, scale=-1.0).then_inc(elog_ready, 1)
            silu(0, EP - 1)
            with act.Fori(1, NG) as g:
                for q in range(EP):
                    silu(g, q)
                    if q == 0:
                        weights_out(g, ps_back)

        @block.gpsimd
        def _(pool):
            nc.gpsimd.memset(minus_half[:, :], -0.5).then_inc(half_set, 1)
            nc.gpsimd.memset(v_blk[:, :, :, :], 0.0).then_inc(v_set, 1)
            pool.wait_ge(v_set, 1)
            nc.gpsimd.memset(v_blk[0:64, :, :, 16:17], 1.0).then_inc(v_set, 1)
            nc.gpsimd.memset(v_blk[64:128, :, :, 17:18], 1.0).then_inc(v_set, 1)
            pool.wait_ge(v_set, 3)
            nc.gpsimd.memset(q_blk[:, :, :, :], 0.0).then_inc(q_zeroed, 1)
            pool.wait_ge(half_set, 1)

            def rstd1_of(c):
                pool.wait_ge(var1_ready, c + 1)
                k = slice(*X_CHUNKS[c])
                nc.gpsimd.tensor_tensor(rstd1[:, k], var1[:, k], minus_half[:, k], ALU.pow).then_inc(rstd1_ready, 1)

            def weights_lo(k):
                pool.wait_ge(whi_ready, 1 if k < 2 else 3)
                w = slice(512 * (k % 2), 512 * (k % 2) + 512)
                f, hi, lo = ((wg_f, wg_hi, wg_lo), (wu_f, wu_hi, wu_lo))[k // 2]
                nc.gpsimd.tensor_tensor(lo[:, w], f[:, w], hi[:, w].bitcast(F32), ALU.subtract).then_inc(wlo_ready, 1)

            def expand(u, j):
                if past(u, 0):
                    pool.wait_ge(scores_done, 4 * u + 2 * j + 2)
                nc.gpsimd.tensor_tensor(k_exp[:, j, :, :, :],
                                        kT[:, j, :, :].unsqueeze(2).broadcast_to([P, 2, HH, S]),
                                        head_mask[:, :].unsqueeze(1).unsqueeze(3).broadcast_to([P, 2, HH, S]),
                                        ALU.mult).then_inc(k_exp_ready, 2 if step_is(u, -1) else 1)

            def step(u):
                if live(u, -2):
                    pool.wait_ge(var2_ready, u - 1)
                    nc.gpsimd.tensor_tensor(rstd2[:, :], var2[:, :], minus_half[:, 0:2], ALU.pow).then_inc(rstd2_ready, 1)
                if step_is(u, 1) or step_is(u, 2):
                    weights_lo(2 * u - 2)
                if live(u, 1):
                    pool.wait_ge(kT_ready, u + 2)
                    if not step_is(u, -1):
                        expand(u, 0)
                if step_is(u, 0):
                    pool.wait_ge(gbo_ready, 1)
                if live(u, 0):
                    tiles = unit_tiles(u)
                    nc.gpsimd.tensor_tensor(x1_all[:, tiles, :], x_all[:, tiles, :],
                                            gbo[:, :].unsqueeze(1).broadcast_to([P, 2, D]), ALU.add).then_inc(xbo_ready, 1)
                if live(u, 1):
                    expand(u, 1)
                if step_is(u, -1):
                    rstd1_of(1)
                    rstd1_of(2)
                if step_is(u, 0):
                    rstd1_of(3)
                if step_is(u, 1) or step_is(u, 2):
                    weights_lo(2 * u - 1)
                if live(u, -2):
                    pool.wait_ge(x2hi_ready, u - 1)
                    cols = bass.ds(UN * (u - 2), UN)
                    nc.gpsimd.tensor_tensor(x2_lo[:, cols], x2T[:, :], x2_hi[:, cols].bitcast(F32),
                                            ALU.subtract).then_inc(x2lo_ready, 1)

            rstd1_of(0)
            nc.gpsimd.memset(combT[:, :].bitcast(F32), 0.0).then_inc(combT_zeroed, 1)
            pool.wait_ge(ld_tables, 16)
            pipeline(pool, step)

        @block.vector
        def _(dve):
            links = [0]

            def link(instruction):
                links[0] += 1
                instruction.then_inc(chain, 1)
                dve.wait_ge(chain, links[0])

            def stats1(c):
                dve.wait_ge(ld_x[c], 16)
                for t in range(*X_CHUNKS[c]):
                    last = nc.vector.bn_stats(stats[:, t, :], x_all[:, t, :])
                link(last)
                for t in range(*X_CHUNKS[c]):
                    last = nc.vector.bn_aggr(mv1[:, t, :], stats[:, t, :])
                link(last)
                k = slice(*X_CHUNKS[c])
                nc.vector.tensor_scalar(var1[:, k], mv1[:, k, 1], LN_EPS, None, ALU.add).then_inc(var1_ready, 1)

            stats1(0)

            def masks():
                dve.wait_ge(ld_mask, 16 * 2)
                nc.vector.tensor_scalar(keep[:, 0:2, :], keys_tok[:, 0:2, :], 0.0, None, ALU.not_equal).then_inc(keep_ready, 1)
                dve.wait_ge(ld_tables, 16)
                nc.vector.tensor_scalar(neg_rows[:, :, :], keys_tok[:, :, :], 0.0, neg_col[:, :],
                                        ALU.is_equal, ALU.mult).then_inc(neg_ready, 1)

            def scores_max(u, j, h):
                dve.wait_ge(scores_done, 4 * u + 2 * j + h + 1)
                nc.vector.tensor_reduce(s_max[:, j, HH * h:HH * h + HH],
                                        ps[j][:, h, :].rearrange("p (h k) -> p h k", k=S),
                                        AX.X, ALU.max).then_inc(max_ready, 1)

            def scores_sub(u, j, h):
                n = 4 * u + 2 * j + h + 1
                dve.wait_ge(max_ready, n)
                if past(u, 1):
                    dve.wait_ge(probs_ready, n - 4)
                nc.vector.tensor_tensor(s_sub[:, j, HH * h:HH * h + HH, :],
                                        ps[j][:, h, :].rearrange("p (h k) -> p h k", k=S),
                                        s_max[:, j, HH * h:HH * h + HH].unsqueeze(2).broadcast_to([P, HH, S]),
                                        ALU.subtract).then_inc(sub_ready, 1)


            def route(g):
                n = [0]

                def done(instruction):
                    n[0] += 1
                    instruction.then_inc(route_step, 1)

                def then():
                    dve.wait_ge(route_step, ROUTE_STEPS * g + n[0])

                tiles = bass.ds(GT * g, GT)
                dve.wait_ge(elog_ready, 2 * g + 2 if isinstance(g, int) else NU + 1)
                if past(g, 1):
                    dve.wait_ge(parts_turned, g)
                done(nc.vector.tensor_scalar(r_den[:, :, :], exp_logit[:, tiles, :], 1.0, None, ALU.add))
                then()
                done(nc.vector.reciprocal(score[:, :, :], r_den[:, :, :]))
                then()
                done(nc.vector.tensor_tensor(choice[:, :, :], score[:, :, :],
                                             rbias[:, :].unsqueeze(1).broadcast_to([P, GT, E]), ALU.add))
                then()
                yield
                quad = choice[:, :, :].rearrange("p t (g a c) -> p (t g) a c", a=2, c=2)
                done(nc.vector.tensor_tensor(pair_hi[:, :, :], quad[:, :, :, 0], quad[:, :, :, 1], ALU.max))
                done(nc.vector.tensor_tensor(pair_lo[:, :, :], quad[:, :, :, 0], quad[:, :, :, 1], ALU.min))
                then()
                done(nc.vector.tensor_tensor(top1[:, :], pair_hi[:, :, 0], pair_hi[:, :, 1], ALU.max))
                done(nc.vector.tensor_tensor(low_hi[:, :], pair_hi[:, :, 0], pair_hi[:, :, 1], ALU.min))
                done(nc.vector.tensor_tensor(hi_low[:, :], pair_lo[:, :, 0], pair_lo[:, :, 1], ALU.max))
                then()
                done(nc.vector.tensor_tensor(top2[:, :], low_hi[:, :], hi_low[:, :], ALU.max))
                then()
                done(nc.vector.tensor_tensor(flat(g_score[:, :, :]), top1[:, :], top2[:, :], ALU.add))
                then()
                yield
                shape = [P, GT, GROUPS, GROUPS]
                other = g_score[:, :, :].unsqueeze(2).broadcast_to(shape)
                own = g_score[:, :, :].unsqueeze(3).broadcast_to(shape)
                done(nc.vector.tensor_tensor(g_ge[:, :, :, :], other, own, ALU.is_ge))
                done(nc.vector.tensor_tensor(g_gt[:, :, :, :], other, own, ALU.is_gt))
                then()
                for k, g_cmp in enumerate((g_ge, g_gt)):
                    done(nc.vector.tensor_tensor(g_cmp[:, :, :, :], g_cmp[:, :, :, :],
                                                 group_order[:, k, :, :].unsqueeze(1).broadcast_to(shape), ALU.mult))
                then()
                done(nc.vector.tensor_tensor(g_ge[:, :, :, :], g_ge[:, :, :, :], g_gt[:, :, :, :], ALU.add))
                then()
                done(nc.vector.tensor_reduce(g_rank[:, :, :], g_ge[:, :, :, :], AX.X, ALU.add))
                then()
                yield
                done(nc.vector.tensor_scalar(g_keep[:, :, :], g_rank[:, :, :], 1.5, None, ALU.is_lt))
                then()
                done(nc.vector.tensor_scalar(g_neg[:, :, :], g_keep[:, :, :], -1.0, -NEG, ALU.add, ALU.mult))
                then()
                c_grp, m_grp = [v[:, :, :].rearrange("p t (g e) -> p (t g) e", g=GROUPS) for v in (choice, masked)]
                k_grp, n_grp = [flat(v[:, :, :]).unsqueeze(2).broadcast_to([P, GT * GROUPS, PER_GROUP])
                                for v in (g_keep, g_neg)]
                done(nc.vector.tensor_tensor(m_grp, c_grp, k_grp, ALU.mult))
                then()
                done(nc.vector.tensor_tensor(m_grp, m_grp, n_grp, ALU.add))
                then()
                done(nc.vector.tensor_copy(rest[:, :, :], masked[:, :, :]))
                yield
                for t in range(GT):
                    done(nc.vector.max(best[:, t, :], masked[:, t, :]))
                then()
                done(nc.vector.memset(best[:, :, TOP_K:8], 3.0e38))
                then()
                done(nc.vector.tensor_copy(w_sel[:, :, :], score[:, :, :]))
                for t in range(GT):
                    done(nc.vector.match_replace(rest[:, t, :], best[:, t, :], masked[:, t, :], -3.0e38))
                then()
                yield
                done(nc.vector.tensor_tensor(chosen[:, :, :], rest[:, :, :], masked[:, :, :], ALU.not_equal))
                then()
                done(nc.vector.tensor_tensor(w_sel[:, :, :], w_sel[:, :, :], chosen[:, :, :], ALU.mult))
                then()
                done(nc.vector.tensor_reduce(w_sum[:, :], w_sel[:, :, :], AX.X, ALU.add))
                then()
                done(nc.vector.tensor_scalar(w_sum[:, :], w_sum[:, :], 1e-20, None, ALU.add))
                then()
                done(nc.vector.reciprocal(w_inv[:, :], w_sum[:, :]))
                then()
                yield
                done(nc.vector.tensor_tensor(comb[:, :, :], w_sel[:, :, :],
                                             w_inv[:, :].unsqueeze(2).broadcast_to([P, GT, E]), ALU.mult))
                then()
                done(nc.vector.tensor_scalar(comb[:, :, :], comb[:, :, :], ROUTED_SCALE, None, ALU.mult))
                then()
                done(nc.vector.tensor_copy(comb_hi[:, :, :], comb[:, :, :]))
                then()
                nc.vector.tensor_copy(comb_parts[:, :, 0, :], comb_hi[:, :, :].bitcast(F32)).then_inc(parts_ready, 1)
                nc.vector.tensor_tensor(comb_parts[:, :, 1, :], comb[:, :, :], comb_hi[:, :, :].bitcast(F32),
                                        ALU.subtract).then_inc(parts_ready, 1)
                assert n[0] == ROUTE_STEPS, n[0]

            def finish(g):
                dve.wait_ge(down_done, EP * (g + 1))
                tiles = bass.ds(GT * g, GT)
                nc.vector.scalar_tensor_tensor(out=flat(y_out[:, tiles, :]), in0=ps_y[:, :], scalar=tgates[:, 1:2],
                                               in1=flat(x1_all[:, tiles, :]), op0=ALU.mult, op1=ALU.add
                                               ).then_inc(y_ready, 1)

            def silu_times_up(g, q):
                n = EP * g + q
                dve.wait_ge(silu_ready, n + 1)
                dve.wait_ge(up_done, n + 1)
                if past(n, 2):
                    dve.wait_ge(hid_ready, n - 1)
                nc.vector.tensor_tensor(gu[:, q % 2, :], silu_g[:, q % 2, :], ps_up[q % 2], ALU.mult).then_inc(gu_ready, 1)

            def weighted(g, q):
                n = EP * g + q
                dve.wait_ge(gu_ready, n + 1)
                dve.wait_ge(comb_done, n + 1)
                if past(n, 4):
                    dve.wait_ge(down_done, n - 3)
                nc.vector.tensor_tensor(hid[:, q % 4, :], gu[:, q % 2, :], ps_comb[q % 2], ALU.mult).then_inc(hid_ready, 1)

            def pair(g, q):
                silu_times_up(g, q)
                weighted(g, q)

            route0, route1 = route(0), route(1)

            def step(u):
                if live(u, 1):
                    if isinstance(u, int) and u < LOOP_FROM:
                        dve.wait_ge(rstd1_ready, min(u + 2, len(X_CHUNKS)))
                    if past(u, 0):
                        dve.wait_ge(xk_done, u + 1)
                    for j in range(2):
                        col = bass.ds(2 * u + 2 + j, 1)
                        last = nc.vector.tensor_scalar(xh[:, j, :], tile_of(x_all, u + 1, j), mv1[:, col, 0], rstd1[:, col],
                                                       ALU.subtract, ALU.mult)
                    last.then_inc(xh_ready, 1)
                if live(u, 0):
                    scores_max(u, 0, 0)
                if live(u, -2):
                    dve.wait_ge(st2_ready, u - 1)
                if live(u, 0):
                    scores_sub(u, 0, 0)
                if live(u, -2):
                    for j in range(2):
                        last = nc.vector.bn_aggr(mv2[:, j, :], stats2[:, j, :])
                    last.then_inc(mv2_ready, 1)
                    dve.wait_ge(mv2_ready, u - 1)
                    nc.vector.tensor_scalar(var2[:, :], mv2[:, :, 1], LN_EPS, None, ALU.add).then_inc(var2_ready, 1)
                if step_is(u, NU - 2) or step_is(u, NU - 1):
                    next(route0)
                if step_is(u, NU):
                    silu_times_up(0, 0)
                    next(route1)
                if step_is(u, NU + 1):
                    pair(0, 2)
                    next(route1)
                if live(u, 0):
                    scores_max(u, 0, 1)
                    scores_sub(u, 0, 1)
                if step_is(u, NU - 2) or step_is(u, NU - 1):
                    next(route0)
                if step_is(u, 0):
                    dve.wait_ge(tanh_ready, 1)
                    nc.vector.tensor_scalar(gbo[:, :], bo_rows[:, :], tgates[:, 0:1], None, ALU.mult).then_inc(gbo_ready, 1)
                if step_is(u, -1):
                    masks()
                if live(u, 1):
                    dve.wait_ge(xT_ready, u + 2)
                    if step_is(u, -1) or step_is(u, 0):
                        dve.wait_ge(keep_ready, u + 2)
                    if past(u, 0):
                        dve.wait_ge(k_exp_ready, 2 * u + 2)
                    for j in range(2):
                        last = nc.vector.tensor_tensor(kT[:, j, :, :],
                                                       f_kT[:, P * j:P * j + P].rearrange("p (a k) -> p a k", a=2),
                                                       tile_of(keep, u + 1, j).unsqueeze(1).broadcast_to([P, 2, S]),
                                                       ALU.mult)
                    last.then_inc(kT_ready, 1)
                if step_is(u, -1):
                    dve.wait_ge(kT_ready, 1)
                    nc.vector.tensor_tensor(k_exp[:, 0, :, :, :],
                                            kT[:, 0, :, :].unsqueeze(2).broadcast_to([P, 2, HH, S]),
                                            head_mask[:, :].unsqueeze(1).unsqueeze(3).broadcast_to([P, 2, HH, S]),
                                            ALU.mult).then_inc(first_k_exp, 1)
                    stats1(1)
                    nc.vector.tensor_scalar(keep[:, 2:NT, :], keys_tok[:, 2:NT, :], 0.0, None, ALU.not_equal
                                            ).then_inc(keep_ready, 1)
                    stats1(2)
                if step_is(u, 0):
                    stats1(3)
                if live(u, -2):
                    dve.wait_ge(rstd2_ready, u - 1)
                    if live(u, -3):
                        dve.wait_ge(x2_turned, u - 2)
                    for j in range(2):
                        last = nc.vector.tensor_scalar(xh2[:, j, :], tile_of(x1_all, u - 2, j), mv2[:, j, 0:1],
                                                       rstd2[:, j:j + 1], ALU.subtract, ALU.mult)
                    last.then_inc(xh2_ready, 1)
                if live(u, 0):
                    scores_max(u, 1, 0)
                if live(u, -1):
                    dve.wait_ge(o_turned, u)
                    o_ps = ps_back[:, :].rearrange("p (n c) -> p n c", c=32)
                    nc.vector.reciprocal(o_inv[:, :, :], o_ps[:, :, 16:18]).then_inc(o_inv_ready, 1)
                    dve.wait_ge(o_inv_ready, u)
                    nc.vector.tensor_tensor(o_tok[:, :, :, :],
                                            o_ps[:, :, 0:16].rearrange("p n (h d) -> p n h d", h=2),
                                            o_inv[:, :, :].unsqueeze(3).broadcast_to([P, 2 * HP, 2, HD]),
                                            ALU.mult).then_inc(o_tok_ready, 1)
                if step_is(u, NU):
                    weighted(0, 0)
                    pair(0, 1)
                    next(route1)
                if step_is(u, NU + 1):
                    pair(0, 3)
                    next(route1)
                if step_is(u, NU + 2):
                    pair(0, 4)
                    next(route1)
                if live(u, 0):
                    scores_sub(u, 1, 0)
                if live(u, 0):
                    if live(u, 1):
                        dve.wait_ge(q_ready, 4 * u + 6)
                    else:
                        dve.wait_ge(qv_done, u + 2)
                    if past(u, 1):
                        dve.wait_ge(pv_done, u)
                    else:
                        dve.wait_ge(v_set, 3)
                    for h2 in range(2):
                        r = slice(64 * h2, 64 * h2 + 64)
                        nc.vector.tensor_copy(v_blk[r, :, :, HD * h2:HD * h2 + HD],
                                              f_v[r, :].rearrange("p (b n d) -> p b n d", n=HP, d=HD)).then_inc(v_ready, 1)
                    if step_is(u, NU - 1):
                        next(route0)
                    scores_max(u, 1, 1)
                if live(u, -1):
                    dve.wait_ge(wo_done, u)
                    dve.wait_ge(xbo_ready, u)
                    tiles = flat(x1_all[:, unit_tiles(u - 1), :])
                    nc.vector.scalar_tensor_tensor(out=tiles, in0=ps_back[:, UN:2 * UN], scalar=tgates[:, 0:1],
                                                   in1=tiles, op0=ALU.mult, op1=ALU.add).then_inc(x1_ready, 1)
                    dve.wait_ge(x1_ready, u)
                if live(u, 0):
                    scores_sub(u, 1, 1)
                if step_is(u, NU + 2):
                    pair(0, 5)
                    next(route1, None)
                if live(u, -1):
                    for j in range(2):
                        last = nc.vector.bn_stats(stats2[:, j, :], tile_of(x1_all, u - 1, j))
                    last.then_inc(st2_ready, 1)
                if step_is(u, NU - 2) or step_is(u, NU - 1):
                    next(route0, None)
                if step_is(u, NU):
                    next(route1)

            pipeline(dve, step)

            def group(g, last):
                stages = iter(()) if last else route(g + 1)
                for q in range(EP):
                    pair(g, q)
                    if q == 1:
                        finish(g - 1)
                    if q < EP - 1:
                        next(stages, None)

            for q in range(FILL, EP):
                pair(0, q)
            with dve.Fori(1, NG - 1) as g:
                group(g, False)
            group(NG - 1, True)
            finish(NG - 1)

        @block.tensor
        def _(pe):
            def turn(dst, src):
                return nc.tensor.transpose(dst, src, ident[:, :])

            def scores(u, j, h):
                n = 4 * u + 2 * j + h + 1
                pe.wait_ge(q_ready, 4 * u + 2 * j + 2)
                if not step_is(u, 0) or j == 1:
                    pe.wait_ge(k_exp_ready, 2 * u + j + 1)
                if past(u, 1):
                    pe.wait_ge(sub_ready, n - 4)
                else:
                    pe.wait_ge(first_k_exp, 1)
                    pe.wait_ge(batch_rows_ready, 1)
                    pe.wait_ge(neg_ready, 1)
                nc.tensor.matmul(ps[j][:, h, :], batch_rows[:, :],
                                 neg_rows[:, bass.ds(2 * u + j, 1), :].broadcast_to([P, HH, S]), start=True, stop=False)
                nc.tensor.matmul(ps[j][:, h, :], q_blk[:, j, h, :], flat(k_exp[:, j, h, :, :]),
                                 start=False, stop=True).then_inc(scores_done, 1)

            def turn_probs(u, j, h):
                n = 4 * u + 2 * j + h + 1
                pe.wait_ge(probs_ready, n)
                if not isinstance(n, int) or n > 2:
                    pe.wait_ge(pT_ready, n - 2)
                for k in range(4):
                    c = 4 * h + k
                    last = turn(ps_pT[h][:, k, :], probs[:, j, P * c:P * c + P])
                last.then_inc(pT_done, 1)

            def turn_weights(g, bank):
                pe.wait_ge(parts_ready, 2 * g + 2)
                if past(g, 1):
                    pe.wait_ge(combT_ready, g)
                for k in range(GT):
                    last = nc.tensor.transpose(bank[0:2 * E, P * k:P * k + P],
                                               comb_parts[:, k, :, :].rearrange("p a e -> p (a e)"), ident[:, :])
                last.then_inc(parts_turned, 1)

            def product3(dst, w_hi, w_lo, c, tok, done):
                w = slice(P * c, P * c + P)
                nc.tensor.matmul(dst, w_lo[:, w], x2_hi[:, tok], start=True, stop=False)
                nc.tensor.matmul(dst, w_hi[:, w], x2_lo[:, tok], start=False, stop=False)
                nc.tensor.matmul(dst, w_hi[:, w], x2_hi[:, tok], start=False, stop=True).then_inc(done, 1)

            def gate(g, q):
                n = EP * g + q
                tok = bass.ds(GN * g, GN)
                if past(n, 2):
                    pe.wait_ge(silu_ready, n - 1)
                product3(ps_gate[q % 2], wg_hi, wg_lo, q, tok, gate_done)

            def up(g, q):
                n = EP * g + q
                tok = bass.ds(GN * g, GN)
                if past(n, 2):
                    pe.wait_ge(gu_ready, n - 1)
                product3(ps_up[q % 2], wu_hi, wu_lo, q, tok, up_done)

            def gate_up(g, q):
                gate(g, q)
                up(g, q)

            def weights(g, q):
                n = EP * g + q
                pe.wait_ge(combT_ready, g + 1)
                if past(n, 2):
                    pe.wait_ge(hid_ready, n - 1)
                nc.tensor.matmul(ps_comb[q % 2], expert_rows[:, q, :], combT[:, bass.ds(GN * g, GN)], start=True, stop=True
                                 ).then_inc(comb_done, 1)

            def down(g, q):
                n = EP * g + q
                pe.wait_ge(hid_ready, n + 1)
                if q == 0 and past(g, 1):
                    pe.wait_ge(y_ready, g)
                for k in range(GT):
                    last = nc.tensor.matmul(ps_y[:, P * k:P * k + P], hid[:, q % 4, P * k:P * k + P], wd[:, q, :],
                                            start=(q == 0 and k == 0), stop=(q == EP - 1), skip_group_check=True)
                last.then_inc(down_done, 1)

            def step(u):
                if live(u, 0):
                    scores(u, 0, 0)
                if step_is(u, NU + 1):
                    down(0, 1)
                    gate_up(0, 4)
                if step_is(u, NU + 2):
                    gate_up(0, 5)
                if live(u, -3):
                    pe.wait_ge(x2T_ready, u - 2)
                    for j in range(2):
                        last = nc.tensor.matmul(ps_back[:, UN + E * j:UN + E * j + E], x2T[:, P * j:P * j + P], rwT[:, :],
                                                start=True, stop=True)
                    last.then_inc(logits_done, 1)
                if step_is(u, NU + 1):
                    weights(0, 4)
                    down(0, 2)
                if step_is(u, NU + 2):
                    weights(0, 5)
                    down(0, 3)
                if live(u, -1):
                    turn_probs(u - 1, 1, 0)
                if step_is(u, NU):
                    pe.wait_ge(sub_ready, 4 * NU - 1)
                    pe.wait_ge(whi_ready, 3)
                    pe.wait_ge(wlo_ready, 4)
                    pe.wait_ge(x2lo_ready, 2)
                    gate_up(0, 0)
                if live(u, 0):
                    scores(u, 0, 1)
                if live(u, -1):
                    turn_probs(u - 1, 1, 1)
                if step_is(u, NU):
                    pe.wait_ge(sub_ready, 4 * NU)
                    gate_up(0, 1)
                if live(u, 1):
                    if past(u, 0):
                        pe.wait_ge(q_ready, 4 * u + 4)
                    if live(u, -1):
                        pe.wait_ge(v_ready, 2 * u)
                    pe.wait_ge(ld_ctx_k, 16 * (u + 2))
                    for half in range(2):
                        for j in range(2):
                            for b in range(2):
                                c = P * j + 64 * half
                                nc.tensor.matmul(f_kT[64 * b:64 * b + 64, c:c + 64], wk[:, 64 * half:64 * half + 64],
                                                 ctx_k[:, j, 64 * b:64 * b + 64], start=True, stop=True)
                    if step_is(u, -1):
                        pe.wait_ge(ld_tables, 16)
                    pe.wait_ge(xh_ready, u + 2)
                    for j in range(2):
                        last = turn(f_xT[:, P * j:P * j + P], xh[:, j, :])
                    last.then_inc(xk_done, 1)
                if live(u, -1):
                    pe.wait_ge(pT_ready, 4 * u)
                    pe.wait_ge(v_ready, 2 * u)
                    if live(u, -3):
                        pe.wait_ge(elog_ready, u - 2)
                    elif live(u, -2):
                        pe.wait_ge(x1_ready, u - 1)
                    for j in range(2):
                        for n in range(HP):
                            for b in range(2):
                                r = 32 * (n % 4)
                                c = UN * j + P * (n // 4) + 64 * b
                                last = nc.tensor.matmul(ps_back[r:r + 32, c:c + 64], v_blk[:, 2 * j + b, n, :],
                                                        pT[:, j, n, 64 * b:64 * b + 64], start=True, stop=True)
                    last.then_inc(pv_done, 1)
                if step_is(u, NU):
                    turn_weights(0, ps_front)
                    gate(0, 2)
                if live(u, 0):
                    scores(u, 1, 0)
                if live(u, -1):
                    pe.wait_ge(oT_ready, u)
                    for k in range(4):
                        last = turn(ps_back[:, P * k:P * k + P], oT[:, k, :])
                    last.then_inc(o_turned, 1)
                if step_is(u, NU):
                    weights(0, 0)
                    up(0, 2)
                    weights(0, 1)
                    gate(0, 3)
                if live(u, 0) or live(u, 1):
                    if live(u, 1):
                        pe.wait_ge(kT_ready, u + 2)
                        pe.wait_ge(xT_ready, u + 2)
                    elif past(u, 1):
                        pe.wait_ge(q_ready, 4 * u + 4)
                        pe.wait_ge(v_ready, 2 * u)
                    if step_is(u, -1):
                        pe.wait_ge(ld_w, 16)
                    if live(u, 0):
                        pe.wait_ge(ld_ctx_v, 16 * (u + 1))
                        for j in range(2):
                            for b in range(2):
                                for h2 in range(2):
                                    c = P * j + 64 * b
                                    last = nc.tensor.matmul(f_v[64 * h2:64 * h2 + 64, c:c + 64],
                                                            ctx_v[:, j, 64 * b:64 * b + 64], v_pair(wv, h2),
                                                            start=True, stop=True)
                    if live(u, 1):
                        for half in range(2):
                            for j in range(2):
                                for b in range(2):
                                    c = P * j + 64 * half
                                    last = nc.tensor.matmul(f_qT[64 * b:64 * b + 64, c:c + 64],
                                                            wq[:, 64 * half:64 * half + 64],
                                                            xT[:, P * j + 64 * b:P * j + 64 * b + 64],
                                                            start=True, stop=True)
                    last.then_inc(qv_done, 1)
                if live(u, -1):
                    pe.wait_ge(o_tok_ready, u)
                    for j in range(2):
                        last = turn(ps_back[:, P * j:P * j + P],
                                    o_tok[:, HP * j:HP * j + HP, :, :].rearrange("p n h d -> p (n h d)"))
                    last.then_inc(on_turned, 1)
                if step_is(u, NU):
                    up(0, 3)
                    weights(0, 2)
                    pe.wait_ge(ld_wd, 16)
                    down(0, 0)
                if live(u, 0):
                    scores(u, 1, 1)
                if live(u, -1):
                    pe.wait_ge(onT_ready, u)
                    if step_is(u, 1):
                        pe.wait_ge(ld_back, 16)
                    for j in range(2):
                        last = nc.tensor.matmul(ps_back[:, UN + P * j:UN + P * j + P], onT[:, j, :], wo[:, :],
                                                start=True, stop=True)
                    last.then_inc(wo_done, 1)
                if step_is(u, NU):
                    weights(0, 3)
                if live(u, 0):
                    turn_probs(u, 0, 0)
                    turn_probs(u, 0, 1)
                if live(u, -2):
                    pe.wait_ge(xh2_ready, u - 1)
                    if live(u, -1):
                        pe.wait_ge(x1_ready, u)
                    else:
                        pe.wait_ge(elog_ready, u - 2)
                    for j in range(2):
                        last = turn(ps_back[:, P * j:P * j + P], xh2[:, j, :])
                    last.then_inc(x2_turned, 1)

            pe.wait_ge(ld_wk, 16)
            pipeline(pe, step)

            def group(g, first):
                for q in range(EP):
                    if not first or q >= FILL:
                        gate_up(g, q)
                        if q == 0:
                            turn_weights(g, ps_back)
                            down(g - 1, EP - 2)
                            weights(g, q)
                        else:
                            weights(g, q)
                            down(*((g, q - 2) if q >= 2 else (g - 1, EP - 1)))

            group(0, True)
            pe.wait_ge(elog_ready, NU)
            pe.wait_ge(x2lo_ready, NU)
            with pe.Fori(1, NG) as g:
                group(g, False)
            down(NG - 1, EP - 2)
            down(NG - 1, EP - 1)


def kernel(**inputs):
    import concourse.bacc as _bacc
    from concourse.bass_utils import run_bass_kernel_spmd as _run

    f = {k: np.asarray(v) for k, v in inputs.items()}
    arrays = {
        "x": f["x"],
        "ctxT": f["ctx_1024"].reshape(B * S, D).T,
        "itok": f["itok_BxS2_0_99"].reshape(NT, 2, S).transpose(1, 0, 2).reshape(2, NT * S),
        "wk": f["L0_xattn_Wk"],
        "w_qv": np.concatenate([f["L0_xattn_Wq"], f["L0_xattn_Wv"]], 1),
        "w_back": np.concatenate([f["L0_xattn_Wo"], f["L0_ffn_router_weight"].T], 1),
        "rows": np.concatenate([f["L0_xattn_bo"], f["L0_ffn_router_bias"], f["g_xattn"], f["g_ffn"]]),
        "wgT": f["L0_ffn_w_gate"].reshape(E * I, D).T,
        "wuT": f["L0_ffn_w_up"].reshape(E * I, D).T,
        "wdT": f["L0_ffn_w_down"].transpose(0, 2, 1).reshape(E * I, D),
    }
    arrays.update(constants())
    arrays = {k: np.ascontiguousarray(v) for k, v in arrays.items()}
    nc = _bacc.Bacc("TRN2", target_bir_lowering=False, num_devices=1)
    aps = {k: nc.dram_tensor(f"in_{k}", v.shape, mybir.dt.from_np(v.dtype), kind="ExternalInput").ap()
           for k, v in arrays.items()}
    out = nc.dram_tensor("out_x", (B, S, D), F32, kind="ExternalOutput").ap()
    build(nc, aps, out)
    r = _run(nc, [{f"in_{k}": v for k, v in arrays.items()}], core_ids=[0])
    return r.results[0]["out_x"]
```

```python
from contextlib import ExitStack

import numpy as np

import concourse.bass as bass
from concourse import mybir

F32 = mybir.dt.float32
F32R = mybir.dt.float32r
BF16 = mybir.dt.bfloat16
I32 = mybir.dt.int32
ALU = mybir.AluOpType
ACT = mybir.ActivationFunctionType
AX = mybir.AxisListType

P = 128
B, S, D = 32, 64, 128
H, HD = 16, 8
E, I = 16, 64
NT = B * S // P
HH = H // 2
HP = H // 2
EP = E // 2
GT = 4
NG = NT // GT
NU = NT // 2
UN = 2 * P
ROUTE_STEPS = 39
LOOP_FROM, LOOP_TO = 3, NU - 2
GN = GT * P
NEG = -1000000000.0
NPIECE = 3
X_CHUNKS = [(0, 2), (2, 4), (4, 6), (6, 10), (10, NT)]
TOKEN_CHUNKS = [(0, 2), (2, 6), (6, NT)]
LN_EPS = 1e-5
SM_SCALE = float(1.0 / np.sqrt(HD))
GROUPS, PER_GROUP, TOP_K = 4, 4, 4
LAG = 3
RING = LAG + 1
FILL = 6
ROUTED_SCALE = 2.5


def neg_pieces():
    rest, out = np.float32(NEG), []
    for _ in range(NPIECE):
        piece = (rest.reshape(1).view(np.uint32) & np.uint32(0xFFFF0000)).view(np.float32)[0]
        out.append(piece)
        rest = np.float32(rest - piece)
    assert rest == 0
    return out


def constants():
    ident = np.eye(P, dtype=np.float32)
    p = np.arange(P)
    head_mask = ((p[:, None] % 64) // HD == np.arange(HH)[None, :]).astype(np.float32)
    neg_col = np.zeros((P, 1), np.float32)
    neg_col[:NPIECE, 0] = neg_pieces()
    expert_rows = np.zeros((P, EP, P), np.float32)
    for q in range(EP):
        for j in range(2):
            for part in range(2):
                expert_rows[16 * part + 2 * q + j, q, 64 * j:64 * j + 64] = 1.0
    g, j = np.arange(GROUPS)[:, None], np.arange(GROUPS)[None, :]
    before = np.broadcast_to((j < g).astype(np.float32), (P, GROUPS, GROUPS))
    after = np.broadcast_to((j > g).astype(np.float32), (P, GROUPS, GROUPS))
    order = np.stack([before, after], 1).reshape(P, -1)
    return {"c_tables": np.concatenate([ident, head_mask, neg_col, order], 1),
            "c_expert_rows": expert_rows.reshape(P, EP * P)}


def build(nc, a, out):
    ctx = ExitStack()
    with ctx:
        def sb(name, shape, dt=F32):
            return ctx.enter_context(nc.sbuf_tensor(name, shape, dt))

        def sem(name):
            return ctx.enter_context(nc.semaphore(name))

        def split(buf, widths):
            ends = np.cumsum(widths).tolist()
            return [buf[:, e - w:e] for e, w in zip(ends, widths)]

        tables = sb("tables", [P, P + HH + 1 + 2 * GROUPS * GROUPS])
        ident, head_mask, neg_col, group_order = split(tables, [P, HH, 1, 2 * GROUPS * GROUPS])
        group_order = group_order.rearrange("p (o g j) -> p o g j", o=2, g=GROUPS)
        ones = sb("ones", [P, P], BF16)
        wk = sb("wk", [P, P])
        w_qv = sb("w_qv", [P, 2 * P])
        wq, wv = split(w_qv, [P, P])
        w_back = sb("w_back", [P, P + E])
        wo, rwT = split(w_back, [P, E])
        rows = sb("rows", [P, P + E + 2])
        bo_rows, rbias, gates = split(rows, [P, E, 2])
        tgates = sb("tgates", [P, 2])
        gbo = sb("gbo", [P, P])
        expert_rows_f = sb("expert_rows_f", [P, EP, P])
        expert_rows = sb("expert_rows", [P, EP, P], F32R)
        wg_f = sb("wg_f", [P, E * I])
        wu_f = sb("wu_f", [P, E * I])
        wg_hi = sb("wg_hi", [P, E * I], F32R)
        wg_lo = sb("wg_lo", [P, E * I], F32R)
        wu_hi = sb("wu_hi", [P, E * I], F32R)
        wu_lo = sb("wu_lo", [P, E * I], F32R)
        wd_f = sb("wd_f", [P, EP, D])
        wd_hi = sb("wd_hi", [P, EP, D], F32R)
        wd_lo = sb("wd_lo", [P, EP, D], F32R)

        x_all = sb("x_all", [P, NT, D])
        x1_all = sb("x1_all", [P, NT, D])
        stats = sb("stats", [P, NT, 6])
        mv1 = sb("mv1", [P, NT, 2])
        var1 = sb("var1", [P, NT])
        rstd1 = sb("rstd1", [P, NT])
        minus_half = sb("minus_half", [P, NT])
        keys_tok = sb("keys_tok", [P, NT, 2, S], I32)
        keep = sb("keep", [P, NT, 2, S])
        neg_rows = sb("neg_rows", [P, NT, 2, S], BF16)
        ctx_k = sb("ctx_k", [P, 2, P])
        ctx_v = sb("ctx_v", [P, 2, P])
        xh = sb("xh", [P, 2, D])
        xT = sb("xT", [P, UN])
        q_blk = sb("q_blk", [P, 2, 2, P])
        kT = sb("kT", [P, 2, 2, S])
        k_exp = sb("k_exp", [P, 2, 2, HH, S])
        v_blk = sb("v_blk", [P, 4, HP, 32])
        s_max = sb("s_max", [P, 2, H])
        s_sub = sb("s_sub", [P, 2, H, S])
        probs = sb("probs", [P, 2, H * S])
        pT = sb("pT", [P, 2, 2 * 4, P])
        oT = sb("oT", [P, 4, P])
        o_inv = sb("o_inv", [P, 2 * HP, 2])
        o_tok = sb("o_tok", [P, 2 * HP, 2, HD])
        onT = sb("onT", [P, 2, P])
        stats2 = sb("stats2", [P, 2, 6])
        mv2 = sb("mv2", [P, 2, 2])
        var2 = sb("var2", [P, 2])
        rstd2 = sb("rstd2", [P, 2])
        xh2 = sb("xh2", [P, 2, D])
        x2T = sb("x2T", [P, UN])
        x2_hi = sb("x2_hi", [P, NT * P], F32R)
        x2_lo = sb("x2_lo", [P, NT * P], F32R)

        exp_logit = sb("exp_logit", [P, NT, E])
        r_den = sb("r_den", [P, GT, E])
        score = sb("score", [P, GT, E])
        choice = sb("choice", [P, GT, E])
        pair_hi = sb("pair_hi", [P, GT * GROUPS, 2])
        pair_lo = sb("pair_lo", [P, GT * GROUPS, 2])
        top1 = sb("top1", [P, GT * GROUPS])
        low_hi = sb("low_hi", [P, GT * GROUPS])
        hi_low = sb("hi_low", [P, GT * GROUPS])
        top2 = sb("top2", [P, GT * GROUPS])
        g_score = sb("g_score", [P, GT, GROUPS])
        g_ge = sb("g_ge", [P, GT, GROUPS, GROUPS])
        g_gt = sb("g_gt", [P, GT, GROUPS, GROUPS])
        g_rank = sb("g_rank", [P, GT, GROUPS])
        g_keep = sb("g_keep", [P, GT, GROUPS])
        g_neg = sb("g_neg", [P, GT, GROUPS])
        masked = sb("masked", [P, GT, E])
        best = sb("best", [P, GT, 8])
        rest = sb("rest", [P, GT, E])
        chosen = sb("chosen", [P, GT, E])
        w_sel = sb("w_sel", [P, GT, E])
        w_sum = sb("w_sum", [P, GT])
        w_inv = sb("w_inv", [P, GT])
        comb = sb("comb", [P, GT, E])
        comb_hi = sb("comb_hi", [P, GT, E], F32R)
        comb_parts = sb("comb_parts", [P, GT, 2, E])
        combT = sb("combT", [P, NG * GN], F32R)

        silu_g = sb("silu_g", [P, 2, GN])
        gu = sb("gu", [P, 2, GN])
        hid = sb("hid", [P, 2, GN])
        hid_hi = sb("hid_hi", [P, RING, GN], F32R)
        hid_lo = sb("hid_lo", [P, RING, GN], F32R)
        yT = sb("yT", [P, GN])
        y_out = sb("y_out", [P, NT, D])

        ps = [ctx.enter_context(nc.psum_tensor(f"ps_scores{i}", [P, 2, 512], F32)) for i in range(2)]
        ps_pT = [ctx.enter_context(nc.psum_tensor(f"ps_pT{i}", [P, 4, P], F32)) for i in range(2)]
        ps_front = ctx.enter_context(nc.psum_tensor("ps_front", [P, 512], F32))
        ps_back = ctx.enter_context(nc.psum_tensor("ps_back", [P, 512], F32))
        f_xT, f_kT = ps_front[:, 0:UN], ps_front[:, UN:2 * UN]
        f_v, f_qT = ps_front[:, 0:UN], ps_front[:, UN:2 * UN]
        ps_gate = [ps[0][:, 0, :], ps[0][:, 1, :]]
        ps_up = [ps[1][:, 0, :], ps[1][:, 1, :]]
        ps_comb = [ps_pT[0][:, :, :].rearrange("p a b -> p (a b)"), ps_pT[1][:, :, :].rearrange("p a b -> p (a b)")]
        ps_yT, ps_turned = ps_front, ps_back
        ps_last = [ps_back[:, :], ps_comb[0]]

        ld_tables, ld_wk, ld_w, ld_mask, ld_mask_rest, ld_rows, ld_back = (
            sem("ld_tables"), sem("ld_wk"), sem("ld_w"), sem("ld_mask"), sem("ld_mask_rest"), sem("ld_rows"), sem("ld_back"))
        ld_moe, ld_wd = sem("ld_moe"), sem("ld_wd")
        ld_x = [sem(f"ld_x{c}") for c in range(len(X_CHUNKS))]
        ld_ctx_k, ld_ctx_v = sem("ld_ctx_k"), sem("ld_ctx_v")
        half_set, q_zeroed, v_set, combT_zeroed = sem("half_set"), sem("q_zeroed"), sem("v_set"), sem("combT_zeroed")
        chain = sem("chain")
        var1_ready, rstd1_ready = sem("var1_ready"), sem("rstd1_ready")
        keep_ready, ones_set, neg_ready, tanh_ready, gbo_ready = (
            sem("keep_ready"), sem("ones_set"), sem("neg_ready"), sem("tanh_ready"), sem("gbo_ready"))
        xh_ready, xk_done, xT_ready, kT_ready, k_exp_ready, first_k_exp = (
            sem("xh_ready"), sem("xk_done"), sem("xT_ready"), sem("kT_ready"), sem("k_exp_ready"), sem("first_k_exp"))
        qv_done, q_ready, v_ready, xbo_ready = sem("qv_done"), sem("q_ready"), sem("v_ready"), sem("xbo_ready")
        scores_done, max_ready, sub_ready, probs_ready = (
            sem("scores_done"), sem("max_ready"), sem("sub_ready"), sem("probs_ready"))
        pT_done, pT_ready = sem("pT_done"), sem("pT_ready")
        pv_done, oT_ready, o_turned, o_inv_ready, o_tok_ready = (
            sem("pv_done"), sem("oT_ready"), sem("o_turned"), sem("o_inv_ready"), sem("o_tok_ready"))
        on_turned, onT_ready, wo_done, x1_ready = sem("on_turned"), sem("onT_ready"), sem("wo_done"), sem("x1_ready")
        st2_ready, mv2_ready, var2_ready, rstd2_ready, xh2_ready = (
            sem("st2_ready"), sem("mv2_ready"), sem("var2_ready"), sem("rstd2_ready"), sem("xh2_ready"))
        x2_turned, x2T_ready, x2hi_ready, x2lo_ready, logits_done, elog_ready = (
            sem("x2_turned"), sem("x2T_ready"), sem("x2hi_ready"), sem("x2lo_ready"), sem("logits_done"), sem("elog_ready"))
        whi_ready, wlo_ready = sem("whi_ready"), sem("wlo_ready")
        parts_ready, parts_turned, combT_ready = sem("parts_ready"), sem("parts_turned"), sem("combT_ready")
        gate_done, up_done, comb_done, silu_ready, gu_ready, hid_ready, down_done = (
            sem("gate_done"), sem("up_done"), sem("comb_done"), sem("silu_ready"), sem("gu_ready"),
            sem("hid_ready"), sem("down_done"))
        hid_hi_ready, hid_lo_ready, last_lo_ready = sem("hid_hi_ready"), sem("hid_lo_ready"), sem("last_lo_ready")
        yT_ready, y_turned, y_ready, y_sent = sem("yT_ready"), sem("y_turned"), sem("y_ready"), sem("y_sent")
        route_step = sem("route_step")

        x_dram = a["x"].rearrange("b s d -> (b s) d").rearrange("(t p) d -> p t d", p=P)
        out_dram = out.rearrange("b s d -> (b s) d").rearrange("(t p) d -> p t d", p=P)
        ctx_dram = a["ctxT"]

        def v_pair(w, h2):
            return w[:, :].rearrange("p (n h d) -> p n h d", h=2, d=HD)[:, :, h2, :]

        block = ctx.enter_context(nc.Block())

        def pipeline(eng, step):
            for u in range(-1, LOOP_FROM):
                step(u)
            with eng.Fori(LOOP_FROM, LOOP_TO) as u:
                step(u)
            for u in range(LOOP_TO, NU + 3):
                step(u)

        def live(u, d):
            return not isinstance(u, int) or 0 <= u + d < NU

        def step_is(u, k):
            return isinstance(u, int) and u == k

        def past(t, k):
            return not isinstance(t, int) or t >= k

        def unit_tiles(u):
            return bass.ds(2 * u, 2)

        def tile_of(buf, u, j):
            return buf[:, bass.ds(2 * u + j, 1), :].squeeze(1)

        def flat(ap):
            return ap.rearrange("p t d -> p (t d)")

        keys_flat = keys_tok[:, :, :, :].rearrange("p t b k -> p (t b k)")

        @block.sync
        def _(sp):
            def load_x(c):
                a_, b_ = X_CHUNKS[c]
                sp.dma_start(x_all[:, a_:b_, :], x_dram[:, a_:b_, :]).then_inc(ld_x[c], 16)

            load_x(0)

            def unit_ctx(u):
                return ctx_dram[:, bass.ds(UN * u, UN)].rearrange("d (t p) -> d t p", t=2)

            def step(u):
                if live(u, 1):
                    if past(u, 0):
                        sp.wait_ge(xk_done, u + 1)
                    sp.dma_start(ctx_k[:, :, :], unit_ctx(u + 1)).then_inc(ld_ctx_k, 16)
                if step_is(u, -1):
                    sp.dma_start(tables[:, :], a["c_tables"]).then_inc(ld_tables, 16)
                    load_x(1)
                    sp.dma_start(ctx_v[:, :, :], unit_ctx(0)).then_inc(ld_ctx_v, 16)
                    sp.dma_start(rows[:, :], a["rows"].partition_broadcast(P)).then_inc(ld_rows, 16)
                    sp.dma_start(keys_flat[:, UN:B * S], a["itok"][0:1, UN:B * S].partition_broadcast(P)
                                 ).then_inc(ld_mask_rest, 16)
                    for c in range(2, len(X_CHUNKS)):
                        load_x(c)
                    sp.dma_start(w_back[:, :], a["w_back"]).then_inc(ld_back, 16)
                if live(u, 0) and not step_is(u, 0):
                    sp.wait_ge(qv_done, u + 1)
                    sp.dma_start(ctx_v[:, :, :], unit_ctx(u)).then_inc(ld_ctx_v, 16)
                if step_is(u, 0):
                    sp.dma_start(wg_f[:, :], a["wgT"]).then_inc(ld_moe, 16)
                    sp.dma_start(wu_f[:, :], a["wuT"]).then_inc(ld_moe, 16)
                    sp.dma_start(expert_rows_f[:, :, :], a["c_expert_rows"].rearrange("p (q c) -> p q c", q=EP)
                                 ).then_inc(ld_moe, 16)
                    sp.dma_start(wd_f[:, :, :], a["wdT"].rearrange("(q p) d -> p q d", p=P)).then_inc(ld_wd, 16)

            pipeline(sp, step)
            with sp.Fori(0, NG - 1) as g:
                sp.wait_ge(y_ready, g + 1)
                sp.dma_start(out_dram[:, bass.ds(GT * g, GT), :], y_out[:, bass.ds(GT * g, GT), :]).then_inc(y_sent, 16)
            for h in range(2):
                sp.wait_ge(y_ready, NG + h)
                t = slice(NT - GT + 2 * h, NT - GT + 2 * h + 2)
                sp.dma_start(out_dram[:, t, :], y_out[:, t, :]).then_inc(y_sent, 16)
            sp.wait_ge(y_sent, 16 * (NG + 1))

        @block.scalar
        def _(act):
            act.dma_start(wk[:, :], a["wk"]).then_inc(ld_wk, 16)
            act.dma_start(keys_flat[:, 0:UN], a["itok"][0:1, 0:UN].partition_broadcast(P)).then_inc(ld_mask, 16)
            act.dma_start(w_qv[:, :], a["w_qv"]).then_inc(ld_w, 16)

            def exp_batch(u, j, b):
                n = 4 * u + 2 * j + b + 1
                act.wait_ge(sub_ready, n)
                if past(u, 1):
                    act.wait_ge(pT_done, n - 4)
                nc.scalar.activation(probs[:, j, 512 * b:512 * b + 512],
                                     flat(s_sub[:, j, HH * b:HH * b + HH, :]),
                                     ACT.Exp, scale=SM_SCALE).then_inc(probs_ready, 1)

            def probs_out(u, j, b):
                act.wait_ge(pT_done, 4 * u + 2 * j + b + 1)
                if past(u, 1):
                    act.wait_ge(pv_done, u)
                nc.scalar.copy(pT[:, j, 4 * b:4 * b + 4, :], ps_pT[b][:, :, :]).then_inc(pT_ready, 1)

            def q_out(u, j):
                if past(u, 0):
                    act.wait_ge(scores_done, 4 * u + 2 * j + 2)
                for half in range(2):
                    r = slice(64 * half, 64 * half + 64)
                    nc.scalar.copy(q_blk[r, j, :, 64 * half:64 * half + 64],
                                   f_qT[r, P * j:P * j + P].rearrange("p (b q) -> p b q", b=2)).then_inc(q_ready, 1)

            def step(u):
                if live(u, -1):
                    exp_batch(u - 1, 1, 1)
                    probs_out(u - 1, 1, 0)
                if live(u, -3):
                    act.wait_ge(logits_done, u - 2)
                    late = step_is(u, NU + 1) or step_is(u, NU + 2)
                    nc.scalar.activation(exp_logit[:, unit_tiles(u - 3), :],
                                         ps_back[:, UN:UN + 2 * E].rearrange("p (t e) -> p t e", t=2),
                                         ACT.Copy if late else ACT.Exp, scale=1.0 if late else -1.0
                                         ).then_inc(elog_ready, 1)
                if live(u, 0):
                    exp_batch(u, 0, 0)
                if live(u, -1):
                    probs_out(u - 1, 1, 1)
                if step_is(u, NU):
                    silu(0, 0)
                    silu(0, 1)
                if live(u, 0):
                    exp_batch(u, 0, 1)
                if live(u, 1):
                    act.wait_ge(xk_done, u + 2)
                    if past(u, 0):
                        act.wait_ge(qv_done, u + 1)
                    nc.scalar.copy(xT[:, :], f_xT).then_inc(xT_ready, 1)
                if live(u, -1):
                    act.wait_ge(pv_done, u)
                    nc.scalar.copy(flat(oT[:, :, :]), ps_back[:, :]).then_inc(oT_ready, 1)
                if step_is(u, 0):
                    act.wait_ge(ld_moe, 16 * 3)
                    nc.scalar.copy(wg_hi[:, :], wg_f[:, :]).then_inc(whi_ready, 1)
                if step_is(u, 1):
                    nc.scalar.copy(wu_hi[:, :], wu_f[:, :]).then_inc(whi_ready, 1)
                if step_is(u, 2):
                    act.wait_ge(ld_wd, 16)
                    nc.scalar.copy(wd_hi[:, :, :], wd_f[:, :, :]).then_inc(whi_ready, 1)
                if step_is(u, NU - 2):
                    nc.scalar.copy(expert_rows[:, :, :], expert_rows_f[:, :, :]).then_inc(whi_ready, 1)
                if step_is(u, NU):
                    act.wait_ge(combT_zeroed, 1)
                    weights_out(0, ps_front)
                    silu(0, 2)
                if live(u, 1):
                    act.wait_ge(qv_done, u + 2)
                    if step_is(u, -1):
                        act.wait_ge(q_zeroed, 1)
                    q_out(u, 0)
                if live(u, -1):
                    act.wait_ge(on_turned, u)
                    nc.scalar.copy(flat(onT[:, :, :]), ps_back[:, 0:UN]).then_inc(onT_ready, 1)
                if step_is(u, NU):
                    hid_high(0, 0)
                    silu(0, 3)
                    hid_high(0, 1)
                if step_is(u, NU + 1):
                    silu(0, 4)
                    hid_high(0, 2)
                if step_is(u, NU + 2):
                    silu(0, 5)
                    hid_high(0, 4)
                if live(u, 0):
                    exp_batch(u, 1, 0)
                if live(u, 1):
                    if live(u, 0):
                        act.wait_ge(v_ready, 2 * u + 2)
                    q_out(u, 1)
                if live(u, 0):
                    probs_out(u, 0, 0)
                    probs_out(u, 0, 1)
                if live(u, -2):
                    act.wait_ge(x2_turned, u - 1)
                    if live(u, -3):
                        act.wait_ge(logits_done, u - 2)
                        act.wait_ge(x2lo_ready, u - 2)
                    nc.scalar.copy(x2T[:, :], ps_back[:, 0:UN]).then_inc(x2T_ready, 1)
                    act.wait_ge(x2T_ready, u - 1)
                    nc.scalar.copy(x2_hi[:, bass.ds(UN * (u - 2), UN)], x2T[:, :]).then_inc(x2hi_ready, 1)
                if step_is(u, NU + 1):
                    hid_high(0, 3)
                if step_is(u, -1):
                    act.wait_ge(ld_rows, 16)
                    nc.scalar.activation(tgates[:, :], gates[:, :], ACT.Tanh).then_inc(tanh_ready, 1)

            def weights_out(g, bank):
                act.wait_ge(parts_turned, g + 1)
                nc.scalar.copy(combT[0:2 * E, bass.ds(GN * g, GN)], bank[0:2 * E, :]).then_inc(combT_ready, 1)

            def silu(g, q):
                n = EP * g + q
                act.wait_ge(gate_done, n + 1)
                if past(n, 2):
                    act.wait_ge(gu_ready, n - 1)
                nc.scalar.activation(silu_g[:, q % 2, :], ps_gate[q % 2], ACT.Silu).then_inc(silu_ready, 1)

            def hid_high(g, q):
                n = EP * g + q
                act.wait_ge(hid_ready, n + 1)
                if past(n, RING):
                    act.wait_ge(down_done, n - RING + 1)
                nc.scalar.copy(hid_hi[:, q % RING, :], hid[:, q % 2, :]).then_inc(hid_hi_ready, 1)

            def yT_out(g):
                act.wait_ge(down_done, EP * (g + 1))
                if past(g, 1):
                    act.wait_ge(y_turned, g)
                nc.scalar.copy(yT[:, :], ps_yT[:, :]).then_inc(yT_ready, 1)

            pipeline(act, step)
            silu(0, FILL)
            late_logits = exp_logit[:, NT - GT:NT, :]
            act.wait_ge(elog_ready, NU)
            nc.scalar.activation(late_logits, late_logits, ACT.Exp, scale=-1.0).then_inc(elog_ready, 1)
            hid_high(0, FILL - 1)
            silu(0, EP - 1)
            hid_high(0, EP - 2)

            def group(g):
                for q in range(EP):
                    if q == LAG:
                        yT_out(g - 1)
                    silu(g, q)
                    if q == 0:
                        weights_out(g, ps_turned)
                        hid_high(g - 1, EP - 1)
                    else:
                        hid_high(g, q - 1)

            group(1)
            with act.Fori(2, NG) as g:
                group(g)
            hid_high(NG - 1, EP - 1)
            act.wait_ge(down_done, EP * NG)
            act.wait_ge(y_turned, NG - 1)
            for h in range(2):
                c = slice(UN * h, UN * h + UN)
                nc.scalar.copy(yT[:, c], ps_yT[:, c]).then_inc(yT_ready, 1)

        @block.gpsimd
        def _(pool):
            nc.gpsimd.memset(minus_half[:, :], -0.5).then_inc(half_set, 1)
            nc.gpsimd.memset(ones[:, :], 1.0).then_inc(ones_set, 1)
            nc.gpsimd.memset(v_blk[:, :, :, :], 0.0).then_inc(v_set, 1)
            pool.wait_ge(v_set, 1)
            nc.gpsimd.memset(v_blk[0:64, :, :, 16:17], 1.0).then_inc(v_set, 1)
            nc.gpsimd.memset(v_blk[64:128, :, :, 17:18], 1.0).then_inc(v_set, 1)
            pool.wait_ge(v_set, 3)
            nc.gpsimd.memset(q_blk[:, :, :, :], 0.0).then_inc(q_zeroed, 1)
            pool.wait_ge(half_set, 1)

            def rstd1_of(c):
                pool.wait_ge(var1_ready, c + 1)
                k = slice(*X_CHUNKS[c])
                nc.gpsimd.tensor_tensor(rstd1[:, k], var1[:, k], minus_half[:, k], ALU.pow).then_inc(rstd1_ready, 1)

            def weights_lo(k):
                pool.wait_ge(whi_ready, k // 2 + 1)
                w = slice(512 * (k % 2), 512 * (k % 2) + 512)
                f, hi, lo = ((wg_f[:, w], wg_hi[:, w], wg_lo[:, w]), (wu_f[:, w], wu_hi[:, w], wu_lo[:, w]),
                             (flat(wd_f[:, :, :])[:, w], flat(wd_hi[:, :, :])[:, w], flat(wd_lo[:, :, :])[:, w]))[k // 2]
                nc.gpsimd.tensor_tensor(lo, f, hi.bitcast(F32), ALU.subtract).then_inc(wlo_ready, 1)

            def hid_low(g, q):
                n = EP * g + q
                pool.wait_ge(hid_hi_ready, n + 1)
                if past(n, RING):
                    pool.wait_ge(down_done, n - RING + 1)
                nc.gpsimd.tensor_tensor(hid_lo[:, q % RING, :], hid[:, q % 2, :], hid_hi[:, q % RING, :].bitcast(F32),
                                        ALU.subtract).then_inc(hid_lo_ready, 1)

            def expand(u, j):
                if past(u, 0):
                    pool.wait_ge(scores_done, 4 * u + 2 * j + 2)
                nc.gpsimd.tensor_tensor(k_exp[:, j, :, :, :],
                                        kT[:, j, :, :].unsqueeze(2).broadcast_to([P, 2, HH, S]),
                                        head_mask[:, :].unsqueeze(1).unsqueeze(3).broadcast_to([P, 2, HH, S]),
                                        ALU.mult).then_inc(k_exp_ready, 2 if step_is(u, -1) else 1)

            def step(u):
                if live(u, -2):
                    pool.wait_ge(var2_ready, u - 1)
                    nc.gpsimd.tensor_tensor(rstd2[:, :], var2[:, :], minus_half[:, 0:2], ALU.pow).then_inc(rstd2_ready, 1)
                if step_is(u, 0):
                    rstd1_of(2)
                if step_is(u, 1) or step_is(u, 2):
                    weights_lo(2 * u - 2)
                if step_is(u, NU - 2):
                    weights_lo(4)
                if step_is(u, NU):
                    hid_low(0, 0)
                    hid_low(0, 1)
                if step_is(u, NU + 1):
                    hid_low(0, 2)
                if step_is(u, NU + 2):
                    hid_low(0, 4)
                if live(u, 1):
                    pool.wait_ge(kT_ready, u + 2)
                    if not step_is(u, -1):
                        expand(u, 0)
                if step_is(u, 1) or step_is(u, 2):
                    rstd1_of(u + 2)
                if step_is(u, 0):
                    pool.wait_ge(gbo_ready, 1)
                if live(u, 0):
                    tiles = unit_tiles(u)
                    nc.gpsimd.tensor_tensor(x1_all[:, tiles, :], x_all[:, tiles, :],
                                            gbo[:, :].unsqueeze(1).broadcast_to([P, 2, D]), ALU.add).then_inc(xbo_ready, 1)
                if live(u, 1):
                    expand(u, 1)
                if step_is(u, -1):
                    rstd1_of(1)
                if step_is(u, 1) or step_is(u, 2):
                    weights_lo(2 * u - 1)
                if step_is(u, NU - 2):
                    weights_lo(5)
                if live(u, -2):
                    pool.wait_ge(x2hi_ready, u - 1)
                    cols = bass.ds(UN * (u - 2), UN)
                    nc.gpsimd.tensor_tensor(x2_lo[:, cols], x2T[:, :], x2_hi[:, cols].bitcast(F32),
                                            ALU.subtract).then_inc(x2lo_ready, 1)
                if step_is(u, NU + 1):
                    hid_low(0, 3)

            rstd1_of(0)
            nc.gpsimd.memset(combT[:, :].bitcast(F32), 0.0).then_inc(combT_zeroed, 1)
            pool.wait_ge(ld_tables, 16)
            pipeline(pool, step)
            for q in range(FILL - 1, EP):
                hid_low(0, q)
            with pool.Fori(1, NG - 1) as g:
                for q in range(EP):
                    hid_low(g, q)
            for q in range(EP - 1):
                hid_low(NG - 1, q)

        @block.vector
        def _(dve):
            links = [0]

            def link(instruction):
                links[0] += 1
                instruction.then_inc(chain, 1)
                dve.wait_ge(chain, links[0])

            def stats1(c):
                dve.wait_ge(ld_x[c], 16)
                for t in range(*X_CHUNKS[c]):
                    last = nc.vector.bn_stats(stats[:, t, :], x_all[:, t, :])
                link(last)
                for t in range(*X_CHUNKS[c]):
                    last = nc.vector.bn_aggr(mv1[:, t, :], stats[:, t, :])
                link(last)
                k = slice(*X_CHUNKS[c])
                nc.vector.tensor_scalar(var1[:, k], mv1[:, k, 1], LN_EPS, None, ALU.add).then_inc(var1_ready, 1)

            stats1(0)

            def find_kept(c):
                t = slice(*TOKEN_CHUNKS[c])
                nc.vector.tensor_scalar(keep[:, t, :, :], keys_tok[:, t, :, :], 0.0, None, ALU.not_equal
                                        ).then_inc(keep_ready, 1)

            def find_padding(c):
                t = slice(*TOKEN_CHUNKS[c])
                nc.vector.tensor_scalar(neg_rows[:, t, :, :], keys_tok[:, t, :, :], 0.0, neg_col[:, :],
                                        ALU.is_equal, ALU.mult).then_inc(neg_ready, 1)

            def scores_max(u, j, b):
                dve.wait_ge(scores_done, 4 * u + 2 * j + b + 1)
                nc.vector.tensor_reduce(s_max[:, j, HH * b:HH * b + HH],
                                        ps[j][:, b, :].rearrange("p (h k) -> p h k", k=S),
                                        AX.X, ALU.max).then_inc(max_ready, 1)

            def scores_sub(u, j, b):
                n = 4 * u + 2 * j + b + 1
                dve.wait_ge(max_ready, n)
                if past(u, 1):
                    dve.wait_ge(probs_ready, n - 4)
                nc.vector.tensor_tensor(s_sub[:, j, HH * b:HH * b + HH, :],
                                        ps[j][:, b, :].rearrange("p (h k) -> p h k", k=S),
                                        s_max[:, j, HH * b:HH * b + HH].unsqueeze(2).broadcast_to([P, HH, S]),
                                        ALU.subtract).then_inc(sub_ready, 1)


            def route(g):
                n = [0]

                def done(instruction):
                    n[0] += 1
                    instruction.then_inc(route_step, 1)

                def then():
                    dve.wait_ge(route_step, ROUTE_STEPS * g + n[0])

                tiles = bass.ds(GT * g, GT)
                dve.wait_ge(elog_ready, 2 * g + 2 if isinstance(g, int) else NU + 1)
                if past(g, 1):
                    dve.wait_ge(parts_turned, g)
                done(nc.vector.tensor_scalar(r_den[:, :, :], exp_logit[:, tiles, :], 1.0, None, ALU.add))
                yield
                then()
                done(nc.vector.reciprocal(score[:, :, :], r_den[:, :, :]))
                yield
                then()
                done(nc.vector.tensor_tensor(choice[:, :, :], score[:, :, :],
                                             rbias[:, :].unsqueeze(1).broadcast_to([P, GT, E]), ALU.add))
                yield
                then()
                quad = choice[:, :, :].rearrange("p t (g a c) -> p (t g) a c", a=2, c=2)
                done(nc.vector.tensor_tensor(pair_hi[:, :, :], quad[:, :, :, 0], quad[:, :, :, 1], ALU.max))
                done(nc.vector.tensor_tensor(pair_lo[:, :, :], quad[:, :, :, 0], quad[:, :, :, 1], ALU.min))
                yield
                then()
                done(nc.vector.tensor_tensor(top1[:, :], pair_hi[:, :, 0], pair_hi[:, :, 1], ALU.max))
                done(nc.vector.tensor_tensor(low_hi[:, :], pair_hi[:, :, 0], pair_hi[:, :, 1], ALU.min))
                done(nc.vector.tensor_tensor(hi_low[:, :], pair_lo[:, :, 0], pair_lo[:, :, 1], ALU.max))
                yield
                then()
                done(nc.vector.tensor_tensor(top2[:, :], low_hi[:, :], hi_low[:, :], ALU.max))
                yield
                then()
                done(nc.vector.tensor_tensor(flat(g_score[:, :, :]), top1[:, :], top2[:, :], ALU.add))
                yield
                then()
                shape = [P, GT, GROUPS, GROUPS]
                other = g_score[:, :, :].unsqueeze(2).broadcast_to(shape)
                own = g_score[:, :, :].unsqueeze(3).broadcast_to(shape)
                done(nc.vector.tensor_tensor(g_ge[:, :, :, :], other, own, ALU.is_ge))
                done(nc.vector.tensor_tensor(g_gt[:, :, :, :], other, own, ALU.is_gt))
                yield
                then()
                for k, g_cmp in enumerate((g_ge, g_gt)):
                    done(nc.vector.tensor_tensor(g_cmp[:, :, :, :], g_cmp[:, :, :, :],
                                                 group_order[:, k, :, :].unsqueeze(1).broadcast_to(shape), ALU.mult))
                yield
                then()
                done(nc.vector.tensor_tensor(g_ge[:, :, :, :], g_ge[:, :, :, :], g_gt[:, :, :, :], ALU.add))
                yield
                then()
                done(nc.vector.tensor_reduce(g_rank[:, :, :], g_ge[:, :, :, :], AX.X, ALU.add))
                yield
                then()
                done(nc.vector.tensor_scalar(g_keep[:, :, :], g_rank[:, :, :], 1.5, None, ALU.is_lt))
                yield
                then()
                done(nc.vector.tensor_scalar(g_neg[:, :, :], g_keep[:, :, :], -1.0, -NEG, ALU.add, ALU.mult))
                yield
                then()
                c_grp, m_grp = [v[:, :, :].rearrange("p t (g e) -> p (t g) e", g=GROUPS) for v in (choice, masked)]
                k_grp, n_grp = [flat(v[:, :, :]).unsqueeze(2).broadcast_to([P, GT * GROUPS, PER_GROUP])
                                for v in (g_keep, g_neg)]
                done(nc.vector.tensor_tensor(m_grp, c_grp, k_grp, ALU.mult))
                yield
                then()
                done(nc.vector.tensor_tensor(m_grp, m_grp, n_grp, ALU.add))
                yield
                then()
                done(nc.vector.tensor_copy(rest[:, :, :], masked[:, :, :]))
                for t in range(GT):
                    done(nc.vector.max(best[:, t, :], masked[:, t, :]))
                yield
                then()
                done(nc.vector.memset(best[:, :, TOP_K:8], 3.0e38))
                yield
                then()
                done(nc.vector.tensor_copy(w_sel[:, :, :], score[:, :, :]))
                for t in range(GT):
                    done(nc.vector.match_replace(rest[:, t, :], best[:, t, :], masked[:, t, :], -3.0e38))
                yield
                then()
                done(nc.vector.tensor_tensor(chosen[:, :, :], rest[:, :, :], masked[:, :, :], ALU.not_equal))
                yield
                then()
                done(nc.vector.tensor_tensor(w_sel[:, :, :], w_sel[:, :, :], chosen[:, :, :], ALU.mult))
                yield
                then()
                done(nc.vector.tensor_reduce(w_sum[:, :], w_sel[:, :, :], AX.X, ALU.add))
                yield
                then()
                done(nc.vector.tensor_scalar(w_sum[:, :], w_sum[:, :], 1e-20, None, ALU.add))
                yield
                then()
                done(nc.vector.reciprocal(w_inv[:, :], w_sum[:, :]))
                yield
                then()
                done(nc.vector.tensor_tensor(comb[:, :, :], w_sel[:, :, :],
                                             w_inv[:, :].unsqueeze(2).broadcast_to([P, GT, E]), ALU.mult))
                yield
                then()
                done(nc.vector.tensor_scalar(comb[:, :, :], comb[:, :, :], ROUTED_SCALE, None, ALU.mult))
                yield
                then()
                done(nc.vector.tensor_copy(comb_hi[:, :, :], comb[:, :, :]))
                yield
                then()
                nc.vector.tensor_copy(comb_parts[:, :, 0, :], comb_hi[:, :, :].bitcast(F32)).then_inc(parts_ready, 1)
                nc.vector.tensor_tensor(comb_parts[:, :, 1, :], comb[:, :, :], comb_hi[:, :, :].bitcast(F32),
                                        ALU.subtract).then_inc(parts_ready, 1)
                assert n[0] == ROUTE_STEPS, n[0]

            def finish(g):
                dve.wait_ge(y_turned, g + 1)
                tiles = bass.ds(GT * g, GT)
                nc.vector.scalar_tensor_tensor(out=flat(y_out[:, tiles, :]), in0=ps_turned[:, :], scalar=tgates[:, 1:2],
                                               in1=flat(x1_all[:, tiles, :]), op0=ALU.mult, op1=ALU.add
                                               ).then_inc(y_ready, 1)

            def routing(steps, k):
                for _ in range(k):
                    next(steps, None)

            def silu_times_up(g, q):
                n = EP * g + q
                dve.wait_ge(silu_ready, n + 1)
                dve.wait_ge(up_done, n + 1)
                if past(n, 2):
                    dve.wait_ge(hid_ready, n - 1)
                nc.vector.tensor_tensor(gu[:, q % 2, :], silu_g[:, q % 2, :], ps_up[q % 2], ALU.mult).then_inc(gu_ready, 1)

            def weighted(g, q):
                n = EP * g + q
                dve.wait_ge(gu_ready, n + 1)
                dve.wait_ge(comb_done, n + 1)
                if past(n, 2):
                    dve.wait_ge(hid_lo_ready, n - 1)
                nc.vector.tensor_tensor(hid[:, q % 2, :], gu[:, q % 2, :], ps_comb[q % 2], ALU.mult).then_inc(hid_ready, 1)

            def pair(g, q):
                silu_times_up(g, q)
                weighted(g, q)

            route0, route1 = route(0), route(1)

            def layernorm2(u):
                dve.wait_ge(rstd2_ready, u - 1)
                if live(u, -3):
                    dve.wait_ge(x2_turned, u - 2)
                for j in range(2):
                    last = nc.vector.tensor_scalar(xh2[:, j, :], tile_of(x1_all, u - 2, j), mv2[:, j, 0:1],
                                                   rstd2[:, j:j + 1], ALU.subtract, ALU.mult)
                last.then_inc(xh2_ready, 1)

            def step(u):
                if live(u, 1):
                    if isinstance(u, int) and u < LOOP_FROM:
                        dve.wait_ge(rstd1_ready, min(u + 2, len(X_CHUNKS)))
                    if past(u, 0):
                        dve.wait_ge(xk_done, u + 1)
                    for j in range(2):
                        col = bass.ds(2 * u + 2 + j, 1)
                        last = nc.vector.tensor_scalar(xh[:, j, :], tile_of(x_all, u + 1, j), mv1[:, col, 0], rstd1[:, col],
                                                       ALU.subtract, ALU.mult)
                    last.then_inc(xh_ready, 1)
                if step_is(u, 0):
                    stats1(2)
                if live(u, 0):
                    scores_max(u, 0, 0)
                if live(u, -2):
                    dve.wait_ge(st2_ready, u - 1)
                if live(u, 0):
                    scores_sub(u, 0, 0)
                if live(u, -2):
                    for j in range(2):
                        last = nc.vector.bn_aggr(mv2[:, j, :], stats2[:, j, :])
                    last.then_inc(mv2_ready, 1)
                    dve.wait_ge(mv2_ready, u - 1)
                    nc.vector.tensor_scalar(var2[:, :], mv2[:, :, 1], LN_EPS, None, ALU.add).then_inc(var2_ready, 1)
                if step_is(u, NU - 2) or step_is(u, NU - 1):
                    routing(route0, 2)
                if step_is(u, NU):
                    routing(route0, ROUTE_STEPS)
                    silu_times_up(0, 0)
                    routing(route1, 5)
                if step_is(u, NU + 1):
                    weighted(0, 2)
                    routing(route1, 4)
                if live(u, 0):
                    scores_max(u, 0, 1)
                    scores_sub(u, 0, 1)
                if step_is(u, NU - 2) or step_is(u, NU - 1):
                    routing(route0, 1)
                if step_is(u, 1) or step_is(u, 2):
                    stats1(u + 2)
                if step_is(u, 0):
                    dve.wait_ge(tanh_ready, 1)
                    nc.vector.tensor_scalar(gbo[:, :], bo_rows[:, :], tgates[:, 0:1], None, ALU.mult).then_inc(gbo_ready, 1)
                if step_is(u, -1):
                    dve.wait_ge(ld_mask, 16)
                    dve.wait_ge(ld_tables, 16)
                    find_kept(0)
                    find_padding(0)
                if live(u, 1):
                    dve.wait_ge(xT_ready, u + 2)
                    if step_is(u, -1) or step_is(u, 0) or step_is(u, 2):
                        dve.wait_ge(keep_ready, min(u + 2, len(TOKEN_CHUNKS)))
                    if past(u, 0):
                        dve.wait_ge(k_exp_ready, 2 * u + 2)
                    nc.vector.tensor_tensor(kT[:, :, :, :].rearrange("p t b k -> p (t b) k"),
                                            f_kT.rearrange("p (a k) -> p a k", k=S),
                                            keep[:, unit_tiles(u + 1), :, :].rearrange("p t b k -> p (t b) k"),
                                            ALU.mult).then_inc(kT_ready, 1)
                if step_is(u, -1):
                    dve.wait_ge(kT_ready, 1)
                    nc.vector.tensor_tensor(k_exp[:, 0, :, :, :],
                                            kT[:, 0, :, :].unsqueeze(2).broadcast_to([P, 2, HH, S]),
                                            head_mask[:, :].unsqueeze(1).unsqueeze(3).broadcast_to([P, 2, HH, S]),
                                            ALU.mult).then_inc(first_k_exp, 1)
                    stats1(1)
                    dve.wait_ge(ld_mask_rest, 16)
                    find_kept(1)
                    find_padding(1)
                if live(u, -2) and not step_is(u, NU):
                    layernorm2(u)
                if step_is(u, 1):
                    find_padding(2)
                if live(u, 0):
                    scores_max(u, 1, 0)
                if live(u, -1):
                    dve.wait_ge(o_turned, u)
                    o_ps = ps_back[:, :].rearrange("p (n c) -> p n c", c=32)
                    nc.vector.reciprocal(o_inv[:, :, :], o_ps[:, :, 16:18]).then_inc(o_inv_ready, 1)
                    dve.wait_ge(o_inv_ready, u)
                    nc.vector.tensor_tensor(o_tok[:, :, :, :],
                                            o_ps[:, :, 0:16].rearrange("p n (h d) -> p n h d", h=2),
                                            o_inv[:, :, :].unsqueeze(3).broadcast_to([P, 2 * HP, 2, HD]),
                                            ALU.mult).then_inc(o_tok_ready, 1)
                if step_is(u, NU):
                    silu_times_up(0, 1)
                    layernorm2(u)
                    weighted(0, 0)
                    weighted(0, 1)
                    silu_times_up(0, 2)
                if step_is(u, NU + 1):
                    pair(0, 3)
                    routing(route1, 4)
                if step_is(u, NU + 2):
                    pair(0, 4)
                    routing(route1, 4)
                if live(u, 0):
                    scores_sub(u, 1, 0)
                if step_is(u, 0):
                    find_kept(2)
                if live(u, 0):
                    if live(u, 1):
                        dve.wait_ge(q_ready, 4 * u + 6)
                    else:
                        dve.wait_ge(qv_done, u + 2)
                    if past(u, 1):
                        dve.wait_ge(pv_done, u)
                    else:
                        dve.wait_ge(v_set, 3)
                    for h2 in range(2):
                        r = slice(64 * h2, 64 * h2 + 64)
                        nc.vector.tensor_copy(v_blk[r, :, :, HD * h2:HD * h2 + HD],
                                              f_v[r, :].rearrange("p (b n d) -> p b n d", n=HP, d=HD)).then_inc(v_ready, 1)
                    scores_max(u, 1, 1)
                if live(u, -1):
                    dve.wait_ge(wo_done, u)
                    dve.wait_ge(xbo_ready, u)
                    tiles = flat(x1_all[:, unit_tiles(u - 1), :])
                    nc.vector.scalar_tensor_tensor(out=tiles, in0=ps_back[:, UN:2 * UN], scalar=tgates[:, 0:1],
                                                   in1=tiles, op0=ALU.mult, op1=ALU.add).then_inc(x1_ready, 1)
                    dve.wait_ge(x1_ready, u)
                if live(u, 0):
                    scores_sub(u, 1, 1)
                if step_is(u, NU + 2):
                    pair(0, 5)
                    routing(route1, 4)
                if live(u, -1):
                    for j in range(2):
                        last = nc.vector.bn_stats(stats2[:, j, :], tile_of(x1_all, u - 1, j))
                    last.then_inc(st2_ready, 1)
                if step_is(u, LOOP_FROM - 1):
                    dve.wait_ge(rstd1_ready, len(X_CHUNKS))
                if step_is(u, NU - 2) or step_is(u, NU - 1):
                    routing(route0, 4)
                if step_is(u, NU):
                    routing(route1, 4)

            pipeline(dve, step)

            def group(g, last):
                following = iter(()) if last else route(g + 1)
                for q in range(EP):
                    routing(following, 1)
                    silu_times_up(g, q)
                    routing(following, 1)
                    weighted(g, q)
                    routing(following, 3)
                    if q == LAG:
                        finish(g - 1)
                routing(following, ROUTE_STEPS)

            for q in range(FILL, EP):
                pair(0, q)
                routing(route1, 6)
            routing(route1, ROUTE_STEPS)
            with dve.Fori(1, NG - 1) as g:
                group(g, False)
            group(NG - 1, True)
            dve.wait_ge(hid_hi_ready, EP * NG)
            dve.wait_ge(down_done, EP * NG - RING)
            q = EP - 1
            nc.vector.tensor_tensor(hid_lo[:, q % RING, :], hid[:, q % 2, :], hid_hi[:, q % RING, :].bitcast(F32),
                                    ALU.subtract).then_inc(last_lo_ready, 1)
            for h in range(2):
                dve.wait_ge(y_turned, NG + h)
                t = slice(NT - GT + 2 * h, NT - GT + 2 * h + 2)
                nc.vector.scalar_tensor_tensor(out=flat(y_out[:, t, :]), in0=ps_last[h][:, 0:UN],
                                               scalar=tgates[:, 1:2], in1=flat(x1_all[:, t, :]),
                                               op0=ALU.mult, op1=ALU.add).then_inc(y_ready, 1)

        @block.tensor
        def _(pe):
            def turn(dst, src):
                return nc.tensor.transpose(dst, src, ident[:, :])

            def scores(u, j, b):
                n = 4 * u + 2 * j + b + 1
                pe.wait_ge(q_ready, 4 * u + 2 * j + 2)
                if not step_is(u, 0) or j == 1:
                    pe.wait_ge(k_exp_ready, 2 * u + j + 1)
                if past(u, 1):
                    pe.wait_ge(sub_ready, n - 4)
                else:
                    pe.wait_ge(first_k_exp, 1)
                    pe.wait_ge(ones_set, 1)
                    pe.wait_ge(neg_ready, 1)
                if step_is(u, 1) or step_is(u, 2):
                    pe.wait_ge(neg_ready, u + 1)
                nc.tensor.matmul(ps[j][:, b, :], ones[:, :],
                                 neg_rows[:, bass.ds(2 * u + j, 1), b, :].broadcast_to([P, HH, S]), start=True, stop=False)
                nc.tensor.matmul(ps[j][:, b, :], q_blk[:, j, b, :], flat(k_exp[:, j, b, :, :]),
                                 start=False, stop=True).then_inc(scores_done, 1)

            def turn_probs(u, j, b):
                n = 4 * u + 2 * j + b + 1
                pe.wait_ge(probs_ready, n)
                if not isinstance(n, int) or n > 2:
                    pe.wait_ge(pT_ready, n - 2)
                for k in range(4):
                    c = 4 * b + k
                    last = turn(ps_pT[b][:, k, :], probs[:, j, P * c:P * c + P])
                last.then_inc(pT_done, 1)

            def turn_weights(g, bank):
                pe.wait_ge(parts_ready, 2 * g + 2)
                if past(g, 1):
                    pe.wait_ge(combT_ready, g)
                for k in range(GT):
                    last = nc.tensor.transpose(bank[0:2 * E, P * k:P * k + P],
                                               comb_parts[:, k, :, :].rearrange("p a e -> p (a e)"), ident[:, :])
                last.then_inc(parts_turned, 1)

            def product3(dst, w_hi, w_lo, c, tok, done):
                w = slice(P * c, P * c + P)
                nc.tensor.matmul(dst, w_lo[:, w], x2_hi[:, tok], start=True, stop=False)
                nc.tensor.matmul(dst, w_hi[:, w], x2_lo[:, tok], start=False, stop=False)
                nc.tensor.matmul(dst, w_hi[:, w], x2_hi[:, tok], start=False, stop=True).then_inc(done, 1)

            def gate(g, q):
                n = EP * g + q
                tok = bass.ds(GN * g, GN)
                if past(n, 2):
                    pe.wait_ge(silu_ready, n - 1)
                product3(ps_gate[q % 2], wg_hi, wg_lo, q, tok, gate_done)

            def up(g, q):
                n = EP * g + q
                tok = bass.ds(GN * g, GN)
                if past(n, 2):
                    pe.wait_ge(gu_ready, n - 1)
                product3(ps_up[q % 2], wu_hi, wu_lo, q, tok, up_done)

            def gate_up(g, q):
                gate(g, q)
                up(g, q)

            def weights(g, q):
                n = EP * g + q
                pe.wait_ge(combT_ready, g + 1)
                if past(n, 2):
                    pe.wait_ge(hid_ready, n - 1)
                nc.tensor.matmul(ps_comb[q % 2], expert_rows[:, q, :], combT[:, bass.ds(GN * g, GN)], start=True, stop=True
                                 ).then_inc(comb_done, 1)

            def down(g, q):
                n = EP * g + q
                pe.wait_ge(hid_hi_ready, n + 1)
                if q == 0 and past(g, 1):
                    pe.wait_ge(yT_ready, g)
                first, last = q == 0, q == EP - 1
                nc.tensor.matmul(ps_yT[:, :], wd_lo[:, q, :], hid_hi[:, q % RING, :], start=first, stop=False)
                nc.tensor.matmul(ps_yT[:, :], wd_hi[:, q, :], hid_hi[:, q % RING, :], start=False, stop=False)
                if isinstance(n, int) and n == EP * NG - 1:
                    pe.wait_ge(last_lo_ready, 1)
                else:
                    pe.wait_ge(hid_lo_ready, n + 1)
                nc.tensor.matmul(ps_yT[:, :], wd_hi[:, q, :], hid_lo[:, q % RING, :], start=False, stop=last
                                 ).then_inc(down_done, 1)

            def turn_y(g):
                pe.wait_ge(yT_ready, g + 1)
                for k in range(GT):
                    last = turn(ps_turned[:, P * k:P * k + P], yT[:, P * k:P * k + P])
                last.then_inc(y_turned, 1)

            def logits(u):
                pe.wait_ge(x2T_ready, u - 2)
                for j in range(2):
                    last = nc.tensor.matmul(ps_back[:, UN + E * j:UN + E * j + E], x2T[:, P * j:P * j + P], rwT[:, :],
                                            start=True, stop=True)
                last.then_inc(logits_done, 1)

            def front(u):
                if past(u, 0):
                    pe.wait_ge(q_ready, 4 * u + 4)
                if live(u, -1):
                    pe.wait_ge(v_ready, 2 * u)
                pe.wait_ge(ld_ctx_k, 16 * (u + 2))
                nc.tensor.matmul(f_kT, wk[:, :], flat(ctx_k[:, :, :]), start=True, stop=True)
                if step_is(u, -1):
                    pe.wait_ge(ld_tables, 16)
                pe.wait_ge(xh_ready, u + 2)
                for j in range(2):
                    last = turn(f_xT[:, P * j:P * j + P], xh[:, j, :])
                last.then_inc(xk_done, 1)

            def values(u):
                pe.wait_ge(pT_ready, 4 * u)
                pe.wait_ge(v_ready, 2 * u)
                if live(u, -3):
                    pe.wait_ge(elog_ready, u - 2)
                elif live(u, -2):
                    pe.wait_ge(x1_ready, u - 1)
                for j in range(2):
                    for n in range(HP):
                        for b in range(2):
                            r = 32 * (n % 4)
                            c = UN * j + P * (n // 4) + 64 * b
                            last = nc.tensor.matmul(ps_back[r:r + 32, c:c + 64], v_blk[:, 2 * j + b, n, :],
                                                    pT[:, j, 4 * b + n % 4, 64 * (n // 4):64 * (n // 4) + 64],
                                                    start=True, stop=True)
                last.then_inc(pv_done, 1)

            def turn_output(u):
                pe.wait_ge(oT_ready, u)
                for k in range(4):
                    last = turn(ps_back[:, P * k:P * k + P], oT[:, k, :])
                last.then_inc(o_turned, 1)

            def v_and_q(u):
                if live(u, 1):
                    pe.wait_ge(kT_ready, u + 2)
                    pe.wait_ge(xT_ready, u + 2)
                elif past(u, 1):
                    pe.wait_ge(q_ready, 4 * u + 4)
                    pe.wait_ge(v_ready, 2 * u)
                if step_is(u, -1):
                    pe.wait_ge(ld_w, 16)
                if live(u, 0):
                    pe.wait_ge(ld_ctx_v, 16 * (u + 1))
                    for j in range(2):
                        for b in range(2):
                            for h2 in range(2):
                                c = P * j + 64 * b
                                last = nc.tensor.matmul(f_v[64 * h2:64 * h2 + 64, c:c + 64],
                                                        ctx_v[:, j, 64 * b:64 * b + 64], v_pair(wv, h2),
                                                        start=True, stop=True)
                if live(u, 1):
                    last = nc.tensor.matmul(f_qT, wq[:, :], xT[:, :], start=True, stop=True)
                last.then_inc(qv_done, 1)

            def turn_normalised(u):
                pe.wait_ge(o_tok_ready, u)
                for j in range(2):
                    last = turn(ps_back[:, P * j:P * j + P],
                                o_tok[:, HP * j:HP * j + HP, :, :].rearrange("p n h d -> p (n h d)"))
                last.then_inc(on_turned, 1)

            def project_output(u):
                pe.wait_ge(onT_ready, u)
                if step_is(u, 1):
                    pe.wait_ge(ld_back, 16)
                for j in range(2):
                    last = nc.tensor.matmul(ps_back[:, UN + P * j:UN + P * j + P], onT[:, j, :], wo[:, :],
                                            start=True, stop=True)
                last.then_inc(wo_done, 1)

            def turn_x2(u):
                pe.wait_ge(xh2_ready, u - 1)
                if live(u, -1):
                    pe.wait_ge(x1_ready, u)
                else:
                    pe.wait_ge(elog_ready, u - 2)
                for j in range(2):
                    last = turn(ps_back[:, P * j:P * j + P], xh2[:, j, :])
                last.then_inc(x2_turned, 1)

            def last_attention(u):
                turn_probs(u - 1, 1, 0)
                logits(u)
                scores(u, 0, 1)
                turn_probs(u - 1, 1, 1)
                scores(u, 1, 0)
                values(u)
                v_and_q(u)
                turn_output(u)
                scores(u, 1, 1)
                turn_normalised(u)
                turn_probs(u, 0, 0)
                project_output(u)
                turn_probs(u, 0, 1)
                turn_x2(u)

            def first_drain(u):
                turn_probs(u - 1, 1, 0)
                pe.wait_ge(sub_ready, 4 * NU - 1)
                pe.wait_ge(whi_ready, 4)
                pe.wait_ge(wlo_ready, 6)
                pe.wait_ge(x2lo_ready, 2)
                gate_up(0, 0)
                logits(u)
                turn_probs(u - 1, 1, 1)
                pe.wait_ge(sub_ready, 4 * NU)
                gate_up(0, 1)
                values(u)
                turn_weights(0, ps_front)
                gate(0, 2)
                turn_output(u)
                weights(0, 0)
                up(0, 2)
                weights(0, 1)
                gate(0, 3)
                turn_normalised(u)
                up(0, 3)
                weights(0, 2)
                project_output(u)
                weights(0, 3)
                turn_x2(u)

            def second_drain(u):
                down(0, 0)
                gate_up(0, 4)
                logits(u)
                weights(0, 4)
                down(0, 1)
                turn_x2(u)

            def third_drain(u):
                gate_up(0, 5)
                logits(u)
                weights(0, 5)
                down(0, 2)

            def step(u):
                if isinstance(u, int) and u >= NU - 1:
                    (last_attention, first_drain, second_drain, third_drain)[u - NU + 1](u)
                    return
                if live(u, -1):
                    turn_probs(u - 1, 1, 0)
                if live(u, -3):
                    logits(u)
                if live(u, 0):
                    scores(u, 0, 1)
                if live(u, -1):
                    turn_probs(u - 1, 1, 1)
                front(u)
                if live(u, -1):
                    values(u)
                if live(u, 0):
                    scores(u, 1, 0)
                if live(u, -1):
                    turn_output(u)
                v_and_q(u)
                if live(u, -1):
                    turn_normalised(u)
                if live(u, 0):
                    scores(u, 1, 1)
                if live(u, -1):
                    project_output(u)
                if live(u, 0):
                    turn_probs(u, 0, 0)
                    turn_probs(u, 0, 1)
                if live(u, -2):
                    turn_x2(u)
                scores(u + 1, 0, 0)

            pe.wait_ge(ld_wk, 16)
            pipeline(pe, step)

            for q in range(FILL, EP):
                gate_up(0, q)
                weights(0, q)
                down(0, q - LAG)
            pe.wait_ge(elog_ready, NU)
            pe.wait_ge(x2lo_ready, NU)
            with pe.Fori(1, NG) as g:
                for q in range(EP):
                    gate(g, q)
                    if q == 0:
                        turn_weights(g, ps_turned)
                    up(g, q)
                    if q == LAG:
                        turn_y(g - 1)
                    if q == EP - 1:
                        weights(g, q)
                    down(*((g, q - LAG) if q >= LAG else (g - 1, EP + q - LAG)))
                    if q < EP - 1:
                        weights(g, q)
            for q in range(EP - LAG, EP):
                down(NG - 1, q)
            for h in range(2):
                pe.wait_ge(yT_ready, NG + h)
                for k in range(2):
                    last = turn(ps_last[h][:, P * k:P * k + P], yT[:, UN * h + P * k:UN * h + P * k + P])
                last.then_inc(y_turned, 1)


def kernel(**inputs):
    import concourse.bacc as _bacc
    from concourse.bass_utils import run_bass_kernel_spmd as _run

    f = {k: np.asarray(v) for k, v in inputs.items()}
    arrays = {
        "x": f["x"],
        "ctxT": f["ctx_1024"].reshape(B * S, D).T,
        "itok": f["itok_BxS2_0_99"].reshape(1, B * S),
        "wk": f["L0_xattn_Wk"],
        "w_qv": np.concatenate([f["L0_xattn_Wq"], f["L0_xattn_Wv"]], 1),
        "w_back": np.concatenate([f["L0_xattn_Wo"], f["L0_ffn_router_weight"].T], 1),
        "rows": np.concatenate([f["L0_xattn_bo"], f["L0_ffn_router_bias"], f["g_xattn"], f["g_ffn"]]),
        "wgT": f["L0_ffn_w_gate"].reshape(E * I, D).T,
        "wuT": f["L0_ffn_w_up"].reshape(E * I, D).T,
        "wdT": f["L0_ffn_w_down"].transpose(0, 2, 1).reshape(E * I, D),
    }
    arrays.update(constants())
    arrays = {k: np.ascontiguousarray(v) for k, v in arrays.items()}
    nc = _bacc.Bacc("TRN2", target_bir_lowering=False, num_devices=1)
    aps = {k: nc.dram_tensor(f"in_{k}", v.shape, mybir.dt.from_np(v.dtype), kind="ExternalInput").ap()
           for k, v in arrays.items()}
    out = nc.dram_tensor("out_x", (B, S, D), F32, kind="ExternalOutput").ap()
    build(nc, aps, out)
    r = _run(nc, [{f"in_{k}": v for k, v in arrays.items()}], core_ids=[0])
    return r.results[0]["out_x"]
```
